# Optimizing a Trainium2 kernel written in Bass

```python
import numpy as np
import jax
import jax.numpy as jnp

def _softmax(x, axis=-1):
    return jax.nn.softmax(x, axis=axis)
def _gelu(x):
    return jax.nn.gelu(x, approximate=True)
def _silu(x):
    return jax.nn.silu(x)
def _sigmoid(x):
    return jax.nn.sigmoid(x)
def _layernorm(x, axis=-1, eps=1e-5):
    m = jnp.mean(x, axis=axis, keepdims=True)
    v = jnp.var(x, axis=axis, keepdims=True)
    return (x - m) / jnp.sqrt(v + eps)
def _scatter_add(tgt, idx, src, axis=0):
    return tgt.at[idx].add(src)
def _segment_sum(src, seg, n):
    return jax.ops.segment_sum(src, seg, n)

kernel_name = 'mk_adj_preln_d1_adj_768_d8fa71'

def setup_inputs(seed: int = 0):
    np.random.seed(seed)
    _w = jnp.asarray
    def _rec_inputs():
        import jax
        import jax.numpy as jnp
        _gk = jax.random.key(seed)
        x = -0.0004039 + 1 * jax.random.normal(jax.random.fold_in(_gk, 1), (128, 64, 768), jnp.float32)
        _w = (1.0 + jnp.arange(64, dtype=jnp.float32)) ** -0.5
        _w = _w / _w.mean()
        _pij = jnp.clip(0.125 * _w[:, None] * _w[None, :], 0.0, 1.0)
        _a = jax.random.uniform(jax.random.fold_in(_gk, 2), (128, 64, 64)) < _pij
        _af = _a.astype(jnp.float32)
        adj = _af
        return x, adj
    x, adj = _rec_inputs()
    def _L0_gnn_setup():
        import jax, jax.numpy as jnp
        import numpy as np
        B, S, H, L = (32, 512, 768, 2)

        def _layer_norm(z, a, b, eps=0.001):
            mu = jnp.mean(z, axis=-1, keepdims=True)
            sigma = jnp.std(z, axis=-1, keepdims=True, ddof=1)
            return (z - mu) / (sigma + eps) * a + b
        key = jax.random.key(seed)
        ks = jax.random.split(key, 6)
        hidden_state = jax.random.normal(ks[0], (B, S, H), dtype=jnp.float32)
        adjacency_matrix = (jax.random.uniform(ks[1], (B, S, S)) < 0.2).astype(jnp.float32)
        W_left = 0.05 * jax.random.normal(ks[2], (L, H, H), dtype=jnp.float32)
        W_right = 0.05 * jax.random.normal(ks[3], (L, H, H), dtype=jnp.float32)
        W_lin = 0.05 * jax.random.normal(ks[4], (L, H, H), dtype=jnp.float32)
        b_lin = jnp.zeros((L, H), dtype=jnp.float32)
        ln_a = jnp.ones((L, H), dtype=jnp.float32)
        ln_b = jnp.zeros((L, H), dtype=jnp.float32)
        return {'hidden_state': hidden_state, 'adjacency_matrix': adjacency_matrix, 'W_left': W_left, 'W_right': W_right, 'W_lin': W_lin, 'b_lin': b_lin, 'ln_a': ln_a, 'ln_b': ln_b}
    _L0_gnn_all = _L0_gnn_setup()
    _L0_gnn_in = {k: v for k, v in _L0_gnn_all.items() if k in ('W_left', 'W_right', 'W_lin', 'b_lin', 'ln_a', 'ln_b', )}
    del _L0_gnn_all

    return {
        "x": x,
        "adj": adj,
        "L0_gnn_W_left": _L0_gnn_in["W_left"],
        "L0_gnn_W_right": _L0_gnn_in["W_right"],
        "L0_gnn_W_lin": _L0_gnn_in["W_lin"],
        "L0_gnn_b_lin": _L0_gnn_in["b_lin"],
        "L0_gnn_ln_a": _L0_gnn_in["ln_a"],
        "L0_gnn_ln_b": _L0_gnn_in["ln_b"],
    }

def reference(x, adj, L0_gnn_W_left, L0_gnn_W_right, L0_gnn_W_lin, L0_gnn_b_lin, L0_gnn_ln_a, L0_gnn_ln_b):
    import jax
    import jax.numpy as jnp
    def _L0_gnn_ref(hidden_state, adjacency_matrix, W_left, W_right, W_lin, b_lin, ln_a, ln_b):
        import jax, jax.numpy as jnp
        import numpy as np
        B, S, H, L = (32, 512, 768, 2)

        def _layer_norm(z, a, b, eps=0.001):
            mu = jnp.mean(z, axis=-1, keepdims=True)
            sigma = jnp.std(z, axis=-1, keepdims=True, ddof=1)
            return (z - mu) / (sigma + eps) * a + b
        temper = float(np.sqrt(H))
        adj = adjacency_matrix
        adj_tri = jnp.triu(adj, k=1)
        diag_mask = jnp.triu(adj, k=0) - adj_tri
        h = hidden_state
        for l in range(L):
            m_left = jnp.einsum('bsh,oh->bso', h, W_left[l])
            m_right = jnp.einsum('bsh,oh->bso', h, W_right[l])
            u_left = jnp.einsum('bih,bjh->bij', h, m_left) / temper
            u_right = jnp.einsum('bih,bjh->bij', h, m_right) / temper
            u = u_left * adj_tri + u_left * diag_mask + u_right * jnp.swapaxes(adj_tri, 1, 2)
            delta_exp_u = jnp.exp(u) * adj
            attention = delta_exp_u / (jnp.sum(delta_exp_u, axis=2, keepdims=True) + 1e-10)
            h_lin = jnp.einsum('bsh,oh->bso', h, W_lin[l]) + b_lin[l]
            ctx = jnp.matmul(attention, h_lin)
            h = jax.nn.relu(_layer_norm(ctx, ln_a[l], ln_b[l]))
        return h

    h = jnp.maximum(_layernorm(x, axis=-1), 0.0)
    x = x + _L0_gnn_ref(h, adj, L0_gnn_W_left, L0_gnn_W_right, L0_gnn_W_lin, L0_gnn_b_lin, L0_gnn_ln_a, L0_gnn_ln_b)
    return x


_drawn_inputs = setup_inputs


def setup_inputs(seed=0):
    import zlib

    import numpy as np

    out = dict(_drawn_inputs(seed))
    spreads = {'L0_gnn_b_lin': (0.0, 0.1), 'L0_gnn_ln_a': (1.0, 0.2), 'L0_gnn_ln_b': (0.0, 0.1)}
    factors = {}
    for name, (base, spread) in spreads.items():
        noise = np.random.default_rng([zlib.crc32(name.encode()), seed]).standard_normal(out[name].shape)
        drawn = base * np.exp(spread * noise) if base else spread * noise
        out[name] = jnp.asarray(drawn.astype(out[name].dtype))
    for name, factor in factors.items():
        out[name] = (out[name] * factor).astype(out[name].dtype)
    return out
```

```python
from contextlib import ExitStack

import concourse.bass as bass
from concourse import mybir

P = 128
F32 = mybir.dt.float32
F16 = mybir.dt.float16
ALU = mybir.AluOpType
ACT = mybir.ActivationFunctionType

W_SCALE = 2.0 ** 6
ATT_SCALE = 2.0 ** 11
LN_X_EPS = 1e-5
LN_EPS = 1e-3
DEN_EPS = 1e-10


def wait(eng, sem, count):
    if isinstance(count, int) and count <= 0:
        return
    eng.wait_ge(sem, count)


def build(nc, x, xt, adj, adjt, wt, b_lin, ln_a, ln_b, out):
    GRAPHS, S, _ = adj.shape
    H = x.shape[1]
    K = H // P
    HALF = H // 2
    PAIRS = 4
    ROWS = PAIRS * P
    GG = 2 * PAIRS
    NGROUP = GRAPHS // GG
    ITER = NGROUP // 2
    TEMPER_INV = 1.0 / float(H) ** 0.5
    STD_FIX = (H / (H - 1.0)) ** 0.5
    MB = 2 * K
    VH = 2 * PAIRS
    TS = 2 * PAIRS
    WCH = 6 * K
    WSLOT = 4

    scratch = nc.dram_tensor("row_stats", [NGROUP, 2, ROWS], F32, kind="Internal").ap()

    with ExitStack() as ctx:
        def sb(name, shape, dt=F32):
            return ctx.enter_context(nc.sbuf_tensor(name, shape, dt))

        def sem(name):
            return ctx.enter_context(nc.semaphore(name))

        w_hi = [sb(f"w_hi{m}", [P, K, H], F16) for m in range(6)]
        w_lo = [sb(f"w_lo{m}", [P, K, H], F16) for m in range(6)]
        ht_hi = [sb(f"ht_hi{i}", [P, K, ROWS], F16) for i in range(2)]
        ht_lo = [sb(f"ht_lo{i}", [P, K, ROWS], F16) for i in range(2)]
        mt_hi = [sb(f"mt_hi{i}", [P, GG, 2, S], F16) for i in range(2)]
        mt_lo = [sb(f"mt_lo{i}", [P, GG, 2, S], F16) for i in range(2)]
        v_hi = sb("v_hi", [P, PAIRS, H], F16)
        v_lo = sb("v_lo", [P, PAIRS, H], F16)
        att_hi = sb("att_hi", [P, PAIRS, P], F16)
        att_lo = sb("att_lo", [P, PAIRS, P], F16)
        norm_rows = [sb(f"norm_rows{i}", [P, H]) for i in range(2)]
        res_rows = [sb(f"res_rows{i}", [P, H]) for i in range(2)]
        stat_rows = sb("stat_rows", [P, H])
        xt_in = [sb(f"xt_in{i}", [P, ROWS]) for i in range(2)]
        bc_stats = sb("bc_stats", [P, 2, ROWS])
        b_lin_bc = [sb(f"b_lin_bc{l}", [P, H]) for l in range(2)]
        a_bc = sb("a_bc", [P, H])
        b_bc = sb("b_bc", [P, H])
        a_col = sb("a_col", [P, K])
        b_col = sb("b_col", [P, K])
        v_sum = [sb(f"v_sum{i}", [P, HALF]) for i in range(2)]
        t_relu = [sb(f"t_relu{i}", [P, 3 * P]) for i in range(2)]
        mask = sb("mask", [P, GG, S])
        adj_e = sb("adj_e", [P, PAIRS, S])
        um = sb("um", [P, GG, S])
        u_shift = sb("u_shift", [P, PAIRS, S])
        e_t = sb("e_t", [P, PAIRS, S])
        den = sb("den", [P, PAIRS, S])
        tri = sb("tri", [P, S])
        ident = sb("ident", [P, P])
        block_ones = sb("block_ones", [P, P])
        half_pow = sb("half_pow", [P, 1])
        neg_half_pow = sb("neg_half_pow", [P, PAIRS])
        x_bn = sb("x_bn", [P, 2, 6])
        x_mv = sb("x_mv", [P, PAIRS, 2])
        x_var = sb("x_var", [P, PAIRS])
        x_stat = sb("x_stat", [P, 2, PAIRS])
        c_bn = sb("c_bn", [P, 2, 6])
        c_mv = sb("c_mv", [P, PAIRS, 2])
        c_sd = sb("c_sd", [P, PAIRS])
        c_den = sb("c_den", [P, PAIRS])
        c_scale = sb("c_scale", [P, PAIRS])
        carrier = sb("carrier", [P, 1])
        c_bias = sb("c_bias", [P, PAIRS])
        w_stage = [res_rows[0], res_rows[1], norm_rows[0], norm_rows[1]]

        ps_w = [ctx.enter_context(nc.psum_tensor(f"ps_w{i}", [P, 512], F32)) for i in range(4)]
        ps_s = ctx.enter_context(nc.psum_tensor("ps_s", [P, GG, S], F32))
        ps_x = ctx.enter_context(nc.psum_tensor("ps_x", [P, 512], F32))
        ps_c = [ctx.enter_context(nc.psum_tensor(f"ps_c{i}", [P, 512], F32)) for i in range(2)]

        s_const = sem("const_in")
        s_w = [sem(f"w_in{i}") for i in range(WSLOT)]
        s_stat_in = sem("stat_rows_in")
        s_xt_in = [sem(f"xt_in_sem{i}") for i in range(2)]
        s_res_in = [sem(f"res_rows_in{i}") for i in range(2)]
        s_out = [sem(f"out_stored{i}") for i in range(2)]
        s_bc_out = sem("row_stats_stored")
        s_bc_in = sem("bc_stats_in")
        s_adj_in = sem("adj_in")
        s_adje_in = sem("adj_e_in")
        s_setup = sem("pool_setup")
        s_clear = sem("att_cleared")
        s_w_hi = sem("w_hi_done")
        s_w_lo = sem("w_lo_done")
        s_x_bn = sem("x_bn_done")
        s_x_mv = sem("x_mv_done")
        s_x_var = sem("x_var_done")
        s_x_stat = sem("x_stat_done")
        s_x_sub = sem("x_sub_done")
        s_x_mul = sem("x_mul_done")
        s_x_hi = sem("x_hi_done")
        s_x_lo = sem("x_lo_done")
        s_m = sem("m_done")
        s_m_hi = sem("m_hi_done")
        s_m_lo = sem("m_lo_done")
        s_s = sem("scores_done")
        s_mask = sem("mask_done")
        s_um = sem("um_done")
        s_shift = sem("u_shift_done")
        s_u = sem("u_done")
        s_exp = sem("exp_done")
        s_e = sem("e_done")
        s_den = sem("den_done")
        s_den_rd = sem("den_read")
        s_recip = sem("recip_done")
        s_att = sem("att_done")
        s_att_hi = sem("att_hi_done")
        s_att_lo = sem("att_lo_done")
        s_v = sem("v_done")
        s_v_sum = sem("v_sum_done")
        s_v_hi = sem("v_hi_done")
        s_v_lo = sem("v_lo_done")
        s_av = sem("av_done")
        s_c_bn = sem("c_bn_done")
        s_c_mv = sem("c_mv_done")
        s_c_sd = sem("c_sd_done")
        s_c_den = sem("c_den_done")
        s_c_scale = sem("c_scale_done")
        s_c_bias = sem("c_bias_done")
        s_norm = sem("norm_done")
        s_t = sem("t_done")
        s_t_relu = sem("t_relu_done")
        s_t_hi = sem("t_hi_done")
        s_t_lo = sem("t_lo_done")
        s_fa = sem("final_a_done")
        s_fb = sem("final_b_done")
        s_f = sem("final_done")

        def all_units(eng, unit):
            unit(0, 0)
            with eng.Fori(0, ITER - 1) as i:
                unit(1, i)
                unit(2, i)
                unit(3, i)
                unit(0, i + 1)
            unit(1, ITER - 1)
            unit(2, ITER - 1)
            unit(3, ITER - 1)

        def has_context(pos, it):
            return not (pos == 0 and isinstance(it, int) and it == 0)

        def transposes(pos):
            return pos in (1, 2)

        def finals(pos, it):
            return pos in (0, 3) and has_context(pos, it)

        def final_group(pos, it):
            return 2 * it if pos == 3 else 2 * it - 1

        def prepares(pos, it):
            return pos == 0 or (pos == 3 and not (isinstance(it, int) and it == ITER - 1))

        def prepared_group(pos, it):
            return 2 * it + 1 if pos == 0 else 2 * it + 2

        def t_before(pos, it):
            return 16 * it + (8 if pos == 2 else 16 if pos == 3 else 0)

        def load_weights(eng, c):
            wait(eng, s_w_lo, c - WSLOT + 1)
            m, k = c // K, c % K
            eng.dma_start(w_stage[c % WSLOT][:], wt[m, k * P:(k + 1) * P, :]).then_inc(s_w[c % WSLOT], 16)

        def first_unit_chunks(step):
            left = WCH - 2 * K
            steps = MB + VH
            if step < K:
                return [2 * K + step]
            return [3 * K + i for i in range((left - K) * (step - K) // (steps - K),
                                             (left - K) * (step - K + 1) // (steps - K))]

        block = ctx.enter_context(nc.Block())

        @block.sync
        def _(sp):
            def load_stat_rows(g, q):
                if q == 0:
                    wait(sp, s_x_lo, K * g)
                else:
                    wait(sp, s_x_mv, 4 * g + q)
                sp.dma_start(stat_rows[:], x[bass.ds(g * ROWS + q * P, P), :]).then_inc(s_stat_in, 16)

            def load_xt(g, k):
                if k != 0:
                    wait(sp, s_x_lo, K * g + k - 1)
                sp.dma_start(xt_in[k % 2][:], xt[k * P:(k + 1) * P, bass.ds(g * ROWS, ROWS)]
                             ).then_inc(s_xt_in[k % 2], 16)

            def spread_stats(g):
                wait(sp, s_x_stat, g * 2 + 2)
                with nc.allow_non_contiguous_dma(reason="8 statistics for each partition"):
                    for w in range(2):
                        sp.dma_start(scratch[bass.ds(g, 1), w, :].rearrange("o (q p) -> p (o q)", p=P),
                                     x_stat[:, w, :]).then_inc(s_bc_out, 16)
                wait(sp, s_bc_out, g * 32 + 32)
                wait(sp, s_x_mul, K * g)
                sp.dma_start(bc_stats[:], scratch[bass.ds(g, 1), :, :].rearrange("o w r -> o (w r)")
                             .broadcast_to([P, 2 * ROWS])).then_inc(s_bc_in, 16)

            def load_res(G, p):
                wait(sp, s_out[p % 2], 32 * G + 16 * (p // 2))
                sp.dma_start(res_rows[p % 2][:], x[bass.ds(G * ROWS + p * P, P), :]).then_inc(s_res_in[p % 2], 16)

            def store(G, p):
                wait(sp, s_f, 4 * G + p + 1)
                sp.dma_start(out[bass.ds(G * ROWS + p * P, P), :], res_rows[p % 2][:]).then_inc(s_out[p % 2], 16)

            def load_adj(pos, it):
                n = 4 * it + pos
                g = 2 * it + pos % 2
                wait(sp, s_um, n)
                sp.dma_start(mask[0:S, :, :], adjt[bass.ds(g * GG, GG), :, :].rearrange("g j i -> j g i")
                             ).then_inc(s_adj_in, 16)
                sp.dma_start(mask[S:P, :, :], adj[bass.ds(g * GG, GG), :, :].rearrange("g j i -> j g i")
                             ).then_inc(s_adj_in, 16)
                wait(sp, s_e, 2 * n)
                of_pair = adjt[bass.ds(g * GG, GG), :, :].rearrange("(p s) j i -> s j p i", s=2)
                for s in range(2):
                    sp.dma_start(adj_e[s * S:(s + 1) * S, :, :], of_pair[s]).then_inc(s_adje_in, 16)

            def unit(pos, it):
                load_adj(pos, it)
                fin, pre = finals(pos, it), prepares(pos, it)
                G, g = final_group(pos, it), prepared_group(pos, it)
                if pre:
                    load_stat_rows(g, 0)
                    load_xt(g, 0)
                    load_xt(g, 1)
                if fin:
                    if pos == 3 and isinstance(it, int) is False:
                        wait(sp, s_w_lo, WCH)
                    load_res(G, 0)
                    load_res(G, 1)
                if pre:
                    load_stat_rows(g, 1)
                    load_stat_rows(g, 2)
                if fin:
                    store(G, 0)
                if pre:
                    load_stat_rows(g, 3)
                if fin:
                    load_res(G, 2)
                    store(G, 1)
                    load_res(G, 3)
                if pre:
                    spread_stats(g)
                if fin:
                    store(G, 2)
                    store(G, 3)
                if pre:
                    for k in range(2, K):
                        load_xt(g, k)

            load_stat_rows(0, 0)
            load_stat_rows(0, 1)
            load_stat_rows(0, 2)
            load_stat_rows(0, 3)
            load_xt(0, 0)
            load_xt(0, 1)
            spread_stats(0)
            for k in range(2, K):
                load_xt(0, k)
            for l in range(2):
                sp.dma_start(b_lin_bc[l][:], b_lin[l:l + 1, :].broadcast_to([P, H])).then_inc(s_const, 16)
            sp.dma_start(a_bc[:], ln_a[1:2, :].broadcast_to([P, H])).then_inc(s_const, 16)
            sp.dma_start(b_bc[:], ln_b[1:2, :].broadcast_to([P, H])).then_inc(s_const, 16)
            with nc.allow_non_contiguous_dma(reason="one layer norm vector down the partitions"):
                sp.dma_start(a_col[:], ln_a[0, :].rearrange("(k p) -> p k", p=P)).then_inc(s_const, 16)
                sp.dma_start(b_col[:], ln_b[0, :].rearrange("(k p) -> p k", p=P)).then_inc(s_const, 16)
            all_units(sp, unit)
            G = NGROUP - 1
            for p in range(PAIRS):
                load_res(G, p)
                if p >= 1:
                    store(G, p - 1)
            store(G, PAIRS - 1)
            for i in range(2):
                wait(sp, s_out[i], 32 * NGROUP)
            wait(sp, s_bc_out, 32 * NGROUP)

        @block.gpsimd
        def _(pool):
            steps = [0]

            def finish(ins):
                steps[0] += 1
                ins.then_inc(s_setup, 1)
                pool.wait_ge(s_setup, steps[0])

            for c in range(WSLOT):
                load_weights(pool, c)
            finish(nc.gpsimd.memset(half_pow[:], 0.5))
            finish(nc.gpsimd.memset(neg_half_pow[:], -0.5))
            finish(nc.gpsimd.memset(tri[:], 1.0))
            finish(nc.gpsimd.memset(ident[:], 0.0))
            finish(nc.gpsimd.affine_select(out=ident[:], in_=ident[:], compare_op=ALU.not_equal, fill=1.0,
                                           base=0, pattern=[[-1, P]], channel_multiplier=1))
            finish(nc.gpsimd.affine_select(out=tri[0:S, :], in_=tri[0:S, :], compare_op=ALU.is_ge, fill=0.0,
                                           base=0, pattern=[[-1, S]], channel_multiplier=1))
            finish(nc.gpsimd.affine_select(out=tri[S:P, :], in_=tri[S:P, :], compare_op=ALU.is_gt, fill=0.0,
                                           base=0, pattern=[[1, S]], channel_multiplier=-1))
            finish(nc.gpsimd.memset(block_ones[:], 0.0))
            finish(nc.gpsimd.memset(block_ones[0:S, 0:S], 1.0))
            finish(nc.gpsimd.memset(block_ones[S:P, S:P], 1.0))

            def x_stats(g):
                wait(pool, s_bc_out, 32 * g)
                pool.wait_ge(s_x_var, g + 1)
                nc.gpsimd.tensor_tensor(x_stat[:, 1, :], x_var[:], neg_half_pow[:], ALU.pow).then_inc(s_x_stat, 1)
                nc.gpsimd.tensor_copy(x_stat[:, 0, :], x_mv[:, :, 0]).then_inc(s_x_stat, 1)

            def context_stats(c, p):
                pool.wait_ge(s_c_mv, c + 1)
                nc.gpsimd.tensor_tensor(c_sd[:, p:p + 1], c_mv[:, p, 1:2], half_pow[:], ALU.pow).then_inc(s_c_sd, 1)

            def unit(pos, it):
                n = 4 * it + pos
                pool.wait_ge(s_adj_in, 32 * n + 32)
                nc.gpsimd.tensor_tensor(mask[:], mask[:], tri[:].unsqueeze(1).broadcast_to([P, GG, S]),
                                        ALU.mult).then_inc(s_mask, 1)
                if not has_context(pos, it):
                    for c in range(2 * K, WCH):
                        load_weights(pool, c)
                        if c == 2 * K + 8:
                            x_stats(prepared_group(pos, it))
                    return
                for j in range(0, MB, 2):
                    if j < 2 * PAIRS:
                        context_stats(4 * (n - 1) + j // 2, j // 2)
                    if j == 8 and prepares(pos, it):
                        x_stats(prepared_group(pos, it))

            x_stats(0)
            for c in range(WSLOT, 2 * K):
                load_weights(pool, c)
            all_units(pool, unit)
            for p in range(PAIRS):
                context_stats(4 * (4 * ITER - 1) + p, p)

        @block.scalar
        def _(act):
            def split_weights(c):
                m, k = c // K, c % K
                act.wait_ge(s_w[c % WSLOT], 16 * (c // WSLOT + 1))
                nc.scalar.activation(w_hi[m][:, k, :], w_stage[c % WSLOT][:], ACT.Copy, scale=W_SCALE
                                     ).then_inc(s_w_hi, 1)

            def x_hi(g, k, buf):
                act.wait_ge(s_x_mul, K * g + k + 1)
                nc.scalar.activation(ht_hi[buf][:, k, :], xt_in[k % 2][:], ACT.Relu).then_inc(s_x_hi, 1)

            def norm(c, p, slot_wait=None):
                act.wait_ge(s_c_bias, c + 1)
                if slot_wait is not None:
                    act.wait_ge(*slot_wait)
                for i in range(2):
                    ins = nc.scalar.activation(norm_rows[p % 2][:, i * HALF:(i + 1) * HALF], ps_c[i][:, 0:HALF],
                                               ACT.Identity, scale=c_scale[:, p:p + 1], bias=c_bias[:, p:p + 1])
                ins.then_inc(s_norm, 1)

            def unit(pos, it):
                n = 4 * it + pos
                t0 = t_before(pos, it)
                first = isinstance(it, int) and n == 0
                for j in range(MB):
                    o, side = j // 2, j % 2
                    act.wait_ge(s_m, MB * n + j + 1)
                    if side == 0:
                        wait(act, s_s, K * n + o - 1)
                    nc.scalar.activation(mt_hi[o % 2][:, :, side, :],
                                         ps_w[j % 4][:].rearrange("f (g r) -> f g r", r=S), ACT.Copy,
                                         scale=1.0 / W_SCALE).then_inc(s_m_hi, 1)
                    if transposes(pos) and 3 <= j < 3 + TS:
                        t = j - 3
                        act.wait_ge(s_t, t0 + t + 1)
                        if t >= 2:
                            act.wait_ge(s_t_lo, t0 + t - 1)
                        for i in range(3):
                            k = 3 * (t % 2) + i
                            ins = nc.scalar.activation(t_relu[t % 2][:, i * P:(i + 1) * P], ps_x[:, i * P:(i + 1) * P],
                                                       ACT.Relu, scale=a_col[:, k:k + 1], bias=b_col[:, k:k + 1])
                        ins.then_inc(s_t_relu, 1)
                    if has_context(pos, it) and j in (2, 4, 6, 8):
                        p = j // 2 - 1
                        if transposes(pos):
                            free = (s_t, t0 + 2 * (p - 1)) if p >= 2 else (s_w_lo, WCH)
                        else:
                            G = final_group(pos, it)
                            free = (s_f, 4 * G + p - 1) if p >= 2 or pos == 0 else None
                        norm(4 * (n - 1) + p, p, free)
                    if first:
                        for c in first_unit_chunks(j):
                            split_weights(c)
                for h in range(VH):
                    act.wait_ge(s_v_sum, VH * n + h + 1)
                    if h == 0:
                        wait(act, s_av, 4 * n)
                    nc.scalar.activation(v_hi[:, h // 2, (h % 2) * HALF:(h % 2 + 1) * HALF], v_sum[h % 2][:],
                                         ACT.Copy).then_inc(s_v_hi, 1)
                    if h == 0:
                        act.wait_ge(s_um, n + 1)
                        nc.scalar.copy(u_shift[0:S, :, :], um[S:P, 0::2, :]).then_inc(s_shift, 1)
                        nc.scalar.copy(u_shift[S:P, :, :], um[0:S, 1::2, :]).then_inc(s_shift, 1)
                        act.wait_ge(s_u, 2 * n + 2)
                        nc.scalar.activation(e_t[:], u_shift[:], ACT.Exp, scale=TEMPER_INV).then_inc(s_exp, 1)
                    if prepares(pos, it) and 1 <= h <= K:
                        if h == 1:
                            wait(act, s_v, VH * n)
                        x_hi(prepared_group(pos, it), h - 1, (pos + 1) % 2)
                    if first:
                        for c in first_unit_chunks(MB + h):
                            split_weights(c)

            for c in range(WSLOT):
                split_weights(c)
            for k in range(K):
                x_hi(0, k, 0)
                for c in range(WSLOT + (2 * K - WSLOT) * k // K, WSLOT + (2 * K - WSLOT) * (k + 1) // K):
                    split_weights(c)
            act.wait_ge(s_const, 6 * 16)
            all_units(act, unit)
            for p in range(PAIRS):
                norm(4 * (4 * ITER - 1) + p, p, (s_f, 4 * (NGROUP - 1) + p - 1))

        @block.vector
        def _(dve):
            def carry_wait():
                nc.vector.memset(carrier[:], 0.0)

            def split_weights(c):
                m, k = c // K, c % K
                dve.wait_ge(s_w_hi, c + 1)
                nc.vector.scalar_tensor_tensor(w_lo[m][:, k, :], w_stage[c % WSLOT][:], W_SCALE, w_hi[m][:, k, :],
                                               ALU.mult, ALU.subtract).then_inc(s_w_lo, 1)

            def x_row_stats(g, q):
                dve.wait_ge(s_stat_in, 64 * g + 16 * q + 16)
                for i in range(2):
                    nc.vector.bn_stats(x_bn[:, i, :], stat_rows[:, i * HALF:(i + 1) * HALF]).then_inc(s_x_bn, 1)
                if q == 0:
                    wait(dve, s_x_stat, 2 * g)
                dve.wait_ge(s_x_bn, 8 * g + 2 * q + 2)
                carry_wait()
                nc.vector.bn_aggr(x_mv[:, q, :], x_bn[:].rearrange("p a b -> p (a b)")).then_inc(s_x_mv, 1)
                if q == PAIRS - 1:
                    dve.wait_ge(s_x_mv, 4 * g + 4)
                    nc.vector.tensor_scalar(x_var[:], x_mv[:, :, 1], LN_X_EPS, None, ALU.add).then_inc(s_x_var, 1)

            def x_norm(g, k):
                dve.wait_ge(s_xt_in[k % 2], 48 * g + 16 * (k // 2) + 16)
                if k == 0:
                    dve.wait_ge(s_bc_in, 16 * g + 16)
                nc.vector.tensor_tensor(xt_in[k % 2][:], xt_in[k % 2][:], bc_stats[:, 0, :], ALU.subtract
                                        ).then_inc(s_x_sub, 1)
                dve.wait_ge(s_x_sub, K * g + k + 1)
                nc.vector.tensor_tensor(xt_in[k % 2][:], xt_in[k % 2][:], bc_stats[:, 1, :], ALU.mult
                                        ).then_inc(s_x_mul, 1)

            def x_lo(g, k, buf):
                dve.wait_ge(s_x_hi, K * g + k + 1)
                nc.vector.scalar_tensor_tensor(ht_lo[buf][:, k, :], xt_in[k % 2][:], 0.0, ht_hi[buf][:, k, :],
                                               ALU.max, ALU.subtract).then_inc(s_x_lo, 1)

            def context_stats(c, p):
                dve.wait_ge(s_av, c + 1)
                for i in range(2):
                    nc.vector.bn_stats(c_bn[:, i, :], ps_c[i][:, 0:HALF]).then_inc(s_c_bn, 1)
                dve.wait_ge(s_c_bn, 2 * c + 2)
                carry_wait()
                nc.vector.bn_aggr(c_mv[:, p, :], c_bn[:].rearrange("p a b -> p (a b)")).then_inc(s_c_mv, 1)

            def context_scale(c, p):
                dve.wait_ge(s_c_sd, c + 1)
                nc.vector.tensor_scalar(c_den[:, p:p + 1], c_sd[:, p:p + 1], STD_FIX, LN_EPS * ATT_SCALE,
                                        ALU.mult, ALU.add).then_inc(s_c_den, 1)
                dve.wait_ge(s_c_den, c + 1)
                nc.vector.reciprocal(c_scale[:, p:p + 1], c_den[:, p:p + 1]).then_inc(s_c_scale, 1)
                dve.wait_ge(s_c_scale, c + 1)
                nc.vector.scalar_tensor_tensor(c_bias[:, p:p + 1], c_mv[:, p, 0:1], -1.0, c_scale[:, p:p + 1],
                                               ALU.mult, ALU.mult).then_inc(s_c_bias, 1)

            def final(c, G, p):
                rows, res = norm_rows[p % 2], res_rows[p % 2]
                dve.wait_ge(s_norm, c + 1)
                nc.vector.tensor_tensor(rows[:], rows[:], a_bc[:], ALU.mult).then_inc(s_fa, 1)
                dve.wait_ge(s_fa, 4 * G + p + 1)
                nc.vector.tensor_tensor(rows[:], rows[:], b_bc[:], ALU.add).then_inc(s_fb, 1)
                dve.wait_ge(s_fb, 4 * G + p + 1)
                dve.wait_ge(s_res_in[p % 2], 32 * G + 16 * (p // 2) + 16)
                nc.vector.scalar_tensor_tensor(res[:], rows[:], 0.0, res[:], ALU.max, ALU.add).then_inc(s_f, 1)

            def v_lo_part(n, h):
                dve.wait_ge(s_v_hi, VH * n + h + 1)
                at = slice((h % 2) * HALF, (h % 2 + 1) * HALF)
                nc.vector.tensor_tensor(v_lo[:, h // 2, at], v_sum[h % 2][:], v_hi[:, h // 2, at], ALU.subtract
                                        ).then_inc(s_v_lo, 1)

            def unit(pos, it):
                n = 4 * it + pos
                t0 = t_before(pos, it)
                layer = pos // 2
                first = isinstance(it, int) and n == 0
                for j in range(MB):
                    o, side = j // 2, j % 2
                    dve.wait_ge(s_m_hi, MB * n + j + 1)
                    nc.vector.scalar_tensor_tensor(mt_lo[o % 2][:, :, side, :],
                                                   ps_w[j % 4][:].rearrange("f (g r) -> f g r", r=S), 1.0 / W_SCALE,
                                                   mt_hi[o % 2][:, :, side, :], ALU.mult, ALU.subtract
                                                   ).then_inc(s_m_lo, 1)
                    if has_context(pos, it) and j in (2, 4, 6, 8):
                        context_scale(4 * (n - 1) + j // 2 - 1, j // 2 - 1)
                    if has_context(pos, it) and j in (1, 3, 5, 7):
                        context_stats(4 * (n - 1) + j // 2, j // 2)
                    if transposes(pos) and 3 <= j < 3 + TS:
                        t = j - 3
                        dve.wait_ge(s_t_relu, t0 + t + 1)
                        if t == 0:
                            wait(dve, s_v, VH * n)
                        to = (slice(None), slice(3 * (t % 2), 3 * (t % 2) + 3), slice(t // 2 * P, (t // 2 + 1) * P))
                        part = t_relu[t % 2][:].rearrange("f (k r) -> f k r", r=P)
                        buf = (pos + 1) % 2
                        nc.vector.tensor_copy(ht_hi[buf][to], part).then_inc(s_t_hi, 1)
                        dve.wait_ge(s_t_hi, t0 + t + 1)
                        nc.vector.tensor_tensor(ht_lo[buf][to], part, ht_hi[buf][to], ALU.subtract
                                                ).then_inc(s_t_lo, 1)
                    if finals(pos, it) and j in (3, 5, 7, 9):
                        p = (j - 3) // 2
                        final(4 * (n - 1) + p, final_group(pos, it), p)
                    if prepares(pos, it) and j in (0, 2, 4, 6):
                        x_row_stats(prepared_group(pos, it), j // 2)
                    if first:
                        for c in first_unit_chunks(j):
                            split_weights(c)
                for h in range(VH):
                    if h >= 1:
                        v_lo_part(n, h - 1)
                    dve.wait_ge(s_v, VH * n + h + 1)
                    nc.vector.scalar_tensor_tensor(v_sum[h % 2][:], ps_w[h % 4][:, 0:HALF], 1.0 / W_SCALE,
                                                   b_lin_bc[layer][:, (h % 2) * HALF:(h % 2 + 1) * HALF],
                                                   ALU.mult, ALU.add).then_inc(s_v_sum, 1)
                    if h == 0:
                        dve.wait_ge(s_s, K * n + K)
                        dve.wait_ge(s_mask, n + 1)
                        nc.vector.tensor_tensor(um[:], ps_s[:], mask[:], ALU.mult).then_inc(s_um, 1)
                        for s in range(2):
                            at = slice(s * S, (s + 1) * S)
                            dve.wait_ge(s_shift, 2 * n + 1 + s)
                            nc.vector.tensor_tensor(u_shift[at, :, :], um[at, s::2, :], u_shift[at, :, :], ALU.add
                                                    ).then_inc(s_u, 1)
                    if h == 1:
                        dve.wait_ge(s_exp, n + 1)
                        dve.wait_ge(s_adje_in, 32 * n + 32)
                        nc.vector.tensor_tensor(e_t[:], e_t[:], adj_e[:], ALU.mult).then_inc(s_e, 2)
                    if h == 4:
                        dve.wait_ge(s_den, n + 1)
                        nc.vector.tensor_scalar(den[:], ps_x[:, 0:PAIRS * S].rearrange("p (a b) -> p a b", b=S),
                                                DEN_EPS, None, ALU.add).then_inc(s_den_rd, 1)
                        dve.wait_ge(s_den_rd, n + 1)
                        nc.vector.reciprocal(den[:], den[:]).then_inc(s_recip, 1)
                        dve.wait_ge(s_recip, n + 1)
                        nc.vector.scalar_tensor_tensor(e_t[:], e_t[:], ATT_SCALE, den[:], ALU.mult, ALU.mult
                                                       ).then_inc(s_att, 1)
                        dve.wait_ge(s_att, n + 1)
                        for s in range(2):
                            at = slice(s * S, (s + 1) * S)
                            nc.vector.tensor_copy(att_hi[at, :, at], e_t[at, :, :]).then_inc(s_att_hi, 1)
                        for s in range(2):
                            at = slice(s * S, (s + 1) * S)
                            dve.wait_ge(s_att_hi, 2 * n + 1 + s)
                            nc.vector.tensor_tensor(att_lo[at, :, at], e_t[at, :, :], att_hi[at, :, at],
                                                    ALU.subtract).then_inc(s_att_lo, 1)
                    if prepares(pos, it):
                        g = prepared_group(pos, it)
                        if 2 <= h <= K + 1:
                            x_lo(g, h - 2, (pos + 1) % 2)
                        if 1 <= h <= K:
                            x_norm(g, h - 1)
                    if first:
                        for c in first_unit_chunks(MB + h):
                            split_weights(c)
                v_lo_part(n, VH - 1)

            nc.vector.memset(att_hi[:], 0.0).then_inc(s_clear, 1)
            nc.vector.memset(att_lo[:], 0.0).then_inc(s_clear, 1)
            dve.wait_ge(s_clear, 2)
            for q in range(PAIRS):
                x_row_stats(0, q)
                split_weights(q)
            for k in range(K):
                x_norm(0, k)
                x_lo(0, k, 0)
                for c in range(WSLOT + (2 * K - WSLOT) * k // K, WSLOT + (2 * K - WSLOT) * (k + 1) // K):
                    split_weights(c)
            dve.wait_ge(s_const, 6 * 16)
            all_units(dve, unit)
            for p in range(PAIRS):
                c = 4 * (4 * ITER - 1) + p
                context_stats(c, p)
                context_scale(c, p)
                final(c, NGROUP - 1, p)

        @block.tensor
        def _(pe):
            def three_passes(ps, pieces, sem, weights_moving=False):
                last = len(pieces) - 1
                for i, (st_hi, st_lo, mv_hi, mv_lo) in enumerate(pieces):
                    nc.tensor.matmul(ps, st_hi, mv_hi, start=(i == 0), stop=False)
                    nc.tensor.matmul(ps, st_hi, mv_lo, start=False, stop=False)
                    ins = nc.tensor.matmul(ps, st_lo, mv_hi, start=False, stop=(i == last))
                if sem is not None:
                    ins.then_inc(sem, 1)

            def scores(n, buf, o):
                pe.wait_ge(s_m_lo, MB * n + 2 * o + 2)
                if o == 0:
                    wait(pe, s_um, n)
                for q in range(GG):
                    at = slice(q * S, (q + 1) * S)
                    m_hi = mt_hi[o % 2][:, q, :, :].rearrange("f s r -> f (s r)")
                    m_lo = mt_lo[o % 2][:, q, :, :].rearrange("f s r -> f (s r)")
                    for i, (m, h) in enumerate(((m_hi, ht_hi), (m_hi, ht_lo), (m_lo, ht_hi))):
                        ins = nc.tensor.matmul(ps_s[:, q, :], m, h[buf][:, o, at],
                                               start=(o == 0 and q == 0 and i == 0), stop=(o == K - 1 and i == 2),
                                               skip_group_check=True)
                ins.then_inc(s_s, 1)

            def context(c, p, n):
                if p == 0:
                    pe.wait_ge(s_att_lo, 2 * n)
                    pe.wait_ge(s_v_lo, VH * n)
                wait(pe, s_norm, c)
                for i in range(2):
                    at = slice(i * HALF, (i + 1) * HALF)
                    three_passes(ps_c[i][:, 0:HALF],
                                 [(att_hi[:, p, :], att_lo[:, p, :], v_hi[:, p, at], v_lo[:, p, at])],
                                 s_av if i == 1 else None)

            def unit(pos, it):
                n = 4 * it + pos
                buf = pos % 2
                layer = pos // 2
                t0 = t_before(pos, it)
                first = isinstance(it, int) and n == 0
                hh, hl = ht_hi[buf], ht_lo[buf]
                if layer == 0:
                    pe.wait_ge(s_x_lo, K * (2 * it + pos) + K)
                else:
                    pe.wait_ge(s_t_lo, 16 * it + (8 if pos == 2 else 16))
                    pe.wait_ge(s_w_lo, WCH)
                for j in range(MB):
                    o, side = j // 2, j % 2
                    m = 3 * layer + side
                    if first and j < 2:
                        pe.wait_ge(s_w_lo, K * (j + 1))
                    if j < 4:
                        wait(pe, s_v_sum, VH * n - 3 + j)
                    else:
                        pe.wait_ge(s_m_lo, MB * n + j - 3)
                    three_passes(ps_w[j % 4][:],
                                 [(w_hi[m][:, k, o * P:(o + 1) * P], w_lo[m][:, k, o * P:(o + 1) * P],
                                   hh[:, k, :], hl[:, k, :]) for k in range(K)], s_m)
                    if side == 1 and o >= 1:
                        scores(n, buf, o - 1)
                    if has_context(pos, it) and j in (1, 3, 5, 7):
                        context(4 * (n - 1) + j // 2, j // 2, n)
                    if transposes(pos) and 3 <= j < 3 + TS:
                        t = j - 3
                        if t % 2 == 0:
                            pe.wait_ge(s_norm, 4 * (n - 1) + t // 2 + 1)
                        if t == 0:
                            pe.wait_ge(s_den_rd, n)
                        else:
                            pe.wait_ge(s_t_relu, t0 + t)
                        for i in range(3):
                            k = 3 * (t % 2) + i
                            ins = nc.tensor.transpose(ps_x[:, i * P:(i + 1) * P],
                                                      norm_rows[(t // 2) % 2][:, k * P:(k + 1) * P], ident[:])
                        ins.then_inc(s_t, 1)
                if first:
                    pe.wait_ge(s_w_lo, 3 * K)
                for h in range(VH):
                    if h < 4:
                        pe.wait_ge(s_m_lo, MB * n + MB - 3 + h)
                    else:
                        pe.wait_ge(s_v_sum, VH * n + h - 3)
                    m = 3 * layer + 2
                    rows = slice(h // 2 * P, (h // 2 + 1) * P)
                    cols = slice((h % 2) * HALF, (h % 2 + 1) * HALF)
                    three_passes(ps_w[h % 4][:, 0:HALF],
                                 [(hh[:, k, rows], hl[:, k, rows], w_hi[m][:, k, cols], w_lo[m][:, k, cols])
                                  for k in range(K)], s_v)
                    if h == 0:
                        scores(n, buf, K - 1)
                    if h == 3:
                        pe.wait_ge(s_e, 2 * n + 2)
                        if transposes(pos):
                            pe.wait_ge(s_t_relu, t0 + TS)
                        else:
                            wait(pe, s_den_rd, n)
                        nc.tensor.matmul(ps_x[:, 0:PAIRS * S], block_ones[:], e_t[:].rearrange("p a b -> p (a b)"),
                                         start=True, stop=True).then_inc(s_den, 1)

            pe.wait_ge(s_setup, 10)
            pe.wait_ge(s_clear, 2)
            all_units(pe, unit)
            for p in range(PAIRS):
                context(4 * (4 * ITER - 1) + p, p, 4 * ITER)


def kernel(**inputs):
    import numpy as np
    import concourse.bacc as bacc
    from concourse.bass_utils import run_bass_kernel_spmd

    x = np.asarray(inputs["x"])
    adj = np.asarray(inputs["adj"])
    B, S, H = x.shape
    rows = np.ascontiguousarray(x.reshape(B * S, H))
    wt = np.stack([np.asarray(inputs[f"L0_gnn_{n}"]) for n in ("W_left", "W_right", "W_lin")], axis=1)
    wt = np.ascontiguousarray(wt.transpose(0, 1, 3, 2).reshape(-1, H, H))
    arrays = {
        "x_rows": rows,
        "x_cols": np.ascontiguousarray(rows.T),
        "adj": np.ascontiguousarray(adj),
        "adj_t": np.ascontiguousarray(adj.transpose(0, 2, 1)),
        "w_t": wt,
        "b_lin": np.ascontiguousarray(inputs["L0_gnn_b_lin"]),
        "ln_a": np.ascontiguousarray(inputs["L0_gnn_ln_a"]),
        "ln_b": np.ascontiguousarray(inputs["L0_gnn_ln_b"]),
    }
    nc = bacc.Bacc("TRN2", target_bir_lowering=False, num_devices=1)
    aps = [nc.dram_tensor(n, a.shape, mybir.dt.from_np(a.dtype), kind="ExternalInput").ap() for n, a in arrays.items()]
    out = nc.dram_tensor("out", (B * S, H), F32, kind="ExternalOutput").ap()
    build(nc, *aps, out)
    r = run_bass_kernel_spmd(nc, [arrays], core_ids=[0])
    return r.results[0]["out"].reshape(B, S, H)
```

```python
from contextlib import ExitStack

import concourse.bass as bass
from concourse import mybir

P = 128
F32 = mybir.dt.float32
F16 = mybir.dt.float16
ALU = mybir.AluOpType
ACT = mybir.ActivationFunctionType

W_SCALE = 2.0 ** 6
ATT_SCALE = 2.0 ** 11
LN_X_EPS = 1e-5
LN_EPS = 1e-3
DEN_EPS = 1e-10


def wait(eng, sem, count):
    if isinstance(count, int) and count <= 0:
        return
    eng.wait_ge(sem, count)


def build(nc, x, xt, adj, adjt, wt, b_lin, ln_a, ln_b, out):
    GRAPHS, S, _ = adj.shape
    H = x.shape[1]
    K = H // P
    HALF = H // 2
    PAIRS = 4
    ROWS = PAIRS * P
    GG = 2 * PAIRS
    NGROUP = GRAPHS // GG
    ITER = NGROUP // 2
    TEMPER_INV = 1.0 / float(H) ** 0.5
    STD_FIX = (H / (H - 1.0)) ** 0.5
    MB = 2 * K
    VH = 2 * PAIRS
    TS = 2 * PAIRS
    X_STEP = 8
    WCH = 6 * K
    WSLOT = 4

    scratch = nc.dram_tensor("row_stats", [NGROUP, 2, ROWS], F32, kind="Internal").ap()

    with ExitStack() as ctx:
        def sb(name, shape, dt=F32):
            return ctx.enter_context(nc.sbuf_tensor(name, shape, dt))

        def sem(name):
            return ctx.enter_context(nc.semaphore(name))

        w_hi = [sb(f"w_hi{m}", [P, K, H], F16) for m in range(6)]
        w_lo = [sb(f"w_lo{m}", [P, K, H], F16) for m in range(6)]
        ht_hi = [sb(f"ht_hi{i}", [P, K, ROWS], F16) for i in range(2)]
        ht_lo = [sb(f"ht_lo{i}", [P, K, ROWS], F16) for i in range(2)]
        mt_hi = [sb(f"mt_hi{i}", [P, GG, 2, S], F16) for i in range(2)]
        mt_lo = [sb(f"mt_lo{i}", [P, GG, 2, S], F16) for i in range(2)]
        v_hi = sb("v_hi", [P, PAIRS, H], F16)
        v_lo = sb("v_lo", [P, PAIRS, H], F16)
        att_hi = sb("att_hi", [P, PAIRS, P], F16)
        att_lo = sb("att_lo", [P, PAIRS, P], F16)
        norm_rows = [sb(f"norm_rows{i}", [P, H]) for i in range(2)]
        res_rows = [sb(f"res_rows{i}", [P, H]) for i in range(2)]
        stat_rows = sb("stat_rows", [P, H])
        xt_in = [sb(f"xt_in{i}", [P, ROWS]) for i in range(2)]
        bc_stats = sb("bc_stats", [P, 2, ROWS])
        b_lin_bc = [sb(f"b_lin_bc{l}", [P, H]) for l in range(2)]
        a_bc = sb("a_bc", [P, H])
        b_bc = sb("b_bc", [P, H])
        a_col = sb("a_col", [P, K])
        b_col = sb("b_col", [P, K])
        v_sum = [sb(f"v_sum{i}", [P, HALF]) for i in range(2)]
        t_relu = [sb(f"t_relu{i}", [P, 3 * P]) for i in range(2)]
        mask = sb("mask", [P, GG, S])
        adj_e = sb("adj_e", [P, PAIRS, S])
        um = sb("um", [P, GG, S])
        u_shift = sb("u_shift", [P, PAIRS, S])
        e_t = sb("e_t", [P, PAIRS, S])
        den = sb("den", [P, PAIRS, S])
        tri = sb("tri", [P, S])
        ident = sb("ident", [P, P])
        block_ones = sb("block_ones", [P, P])
        half_pow = sb("half_pow", [P, 1])
        neg_half_pow = sb("neg_half_pow", [P, PAIRS])
        x_bn = sb("x_bn", [P, PAIRS, 2, 6])
        x_mv = sb("x_mv", [P, PAIRS, 2])
        x_var = sb("x_var", [P, PAIRS])
        x_stat = sb("x_stat", [P, 2, PAIRS])
        c_bn = sb("c_bn", [P, PAIRS, 2, 6])
        c_mv = sb("c_mv", [P, PAIRS, 2])
        c_sd = sb("c_sd", [P, PAIRS])
        c_den = sb("c_den", [P, PAIRS])
        c_scale = sb("c_scale", [P, PAIRS])
        carrier = sb("carrier", [P, 1])
        c_bias = sb("c_bias", [P, PAIRS])
        w_stage = [t[:] for t in (res_rows[0], res_rows[1], norm_rows[0], norm_rows[1])]
        for t in (v_hi, v_lo):
            halves = t[:].rearrange("p a h -> p (a h)").bitcast(F32)
            w_stage += [halves[:, 0:H], halves[:, H:2 * H]]
        x_stage = []
        for t in (ht_hi[1], ht_lo[1]):
            halves = t[:].rearrange("p a h -> p (a h)").bitcast(F32)
            x_stage += [halves[:, 0:H], halves[:, H:2 * H]]

        ps_w = [ctx.enter_context(nc.psum_tensor(f"ps_w{i}", [P, 512], F32)) for i in range(4)]
        ps_s = ctx.enter_context(nc.psum_tensor("ps_s", [P, GG, S], F32))
        ps_s_flat = ps_s[:].rearrange("p g r -> p (g r)")
        ps_x = ctx.enter_context(nc.psum_tensor("ps_x", [P, 512], F32))
        ps_c = [ctx.enter_context(nc.psum_tensor(f"ps_c{i}", [P, 512], F32)) for i in range(2)]

        s_const = sem("const_in")
        s_w = [sem(f"w_in{i}") for i in range(2 * WSLOT)]
        s_x0_in = [sem(f"x_stage_in{i}") for i in range(PAIRS)]
        s_stat_in = sem("stat_rows_in")
        s_xt_in = [sem(f"xt_in_sem{i}") for i in range(2)]
        s_res_in = [sem(f"res_rows_in{i}") for i in range(2)]
        s_out = [sem(f"out_stored{i}") for i in range(2)]
        s_bc_out = sem("row_stats_stored")
        s_bc_in = sem("bc_stats_in")
        s_adj_in = sem("adj_in")
        s_adje_in = sem("adj_e_in")
        s_setup = sem("pool_setup")
        s_clear = sem("att_cleared")
        s_w_hi = sem("w_hi_done")
        s_w_lo = sem("w_lo_done")
        s_x_bn = sem("x_bn_done")
        s_x_mv = sem("x_mv_done")
        s_x_var = sem("x_var_done")
        s_x_stat = sem("x_stat_done")
        s_x_sub = sem("x_sub_done")
        s_x_mul = sem("x_mul_done")
        s_x_hi = sem("x_hi_done")
        s_x_lo = sem("x_lo_done")
        s_m = sem("m_done")
        s_m_hi = sem("m_hi_done")
        s_m_lo = sem("m_lo_done")
        s_s = sem("scores_done")
        s_mask = sem("mask_done")
        s_um = sem("um_done")
        s_shift = sem("u_shift_done")
        s_u = sem("u_done")
        s_exp = sem("exp_done")
        s_e = sem("e_done")
        s_den = sem("den_done")
        s_den_rd = sem("den_read")
        s_recip = sem("recip_done")
        s_att = sem("att_done")
        s_att_hi = sem("att_hi_done")
        s_att_lo = sem("att_lo_done")
        s_v = sem("v_done")
        s_v_sum = sem("v_sum_done")
        s_v_hi = sem("v_hi_done")
        s_v_lo = sem("v_lo_done")
        s_av = sem("av_done")
        s_c_bn = sem("c_bn_done")
        s_c_mv = sem("c_mv_done")
        s_c_sd = sem("c_sd_done")
        s_c_den = sem("c_den_done")
        s_c_scale = sem("c_scale_done")
        s_c_bias = sem("c_bias_done")
        s_norm = sem("norm_done")
        s_t = sem("t_done")
        s_t_relu = sem("t_relu_done")
        s_t_hi = sem("t_hi_done")
        s_t_lo = sem("t_lo_done")
        s_fa = sem("final_a_done")
        s_fb = sem("final_b_done")
        s_f = sem("final_done")

        def all_units(eng, unit):
            unit(0, 0)
            with eng.Fori(0, ITER - 1) as i:
                unit(1, i)
                unit(2, i)
                unit(3, i)
                unit(0, i + 1)
            unit(1, ITER - 1)
            unit(2, ITER - 1)
            unit(3, ITER - 1)

        def has_context(pos, it):
            return not (pos == 0 and isinstance(it, int) and it == 0)

        def transposes(pos):
            return pos in (1, 2)

        def finals(pos, it):
            return pos in (0, 3) and has_context(pos, it)

        def is_last(pos, it):
            return pos == 3 and isinstance(it, int) and it == ITER - 1

        def last_banks(p):
            return (ps_c[0], ps_c[1]) if p % 2 == 0 else (ps_s_flat, ps_x)

        def final_group(pos, it):
            return 2 * it if pos == 3 else 2 * it - 1

        def prepares(pos, it):
            return pos == 0 or (pos == 3 and not (isinstance(it, int) and it == ITER - 1))

        def prepared_group(pos, it):
            return 2 * it + 1 if pos == 0 else 2 * it + 2

        def t_before(pos, it):
            return 16 * it + (8 if pos == 2 else 16 if pos == 3 else 0)

        w_slot = [c % (2 * WSLOT) if c < 4 * WSLOT else c % WSLOT for c in range(WCH)]
        w_before = [max([b for b in range(c) if w_slot[b] == w_slot[c]], default=-1) for c in range(WCH)]
        w_turn = [w_slot[:c + 1].count(w_slot[c]) for c in range(WCH)]

        def load_weights(eng, c):
            wait(eng, s_w_lo, w_before[c] + 1)
            m, k = c // K, c % K
            eng.dma_start(w_stage[w_slot[c]], wt[m, k * P:(k + 1) * P, :]).then_inc(s_w[w_slot[c]], 16)

        def first_unit_chunks(step):
            if step < 8:
                return [2 * K + 2 * step, 2 * K + 2 * step + 1]
            return [2 * K + 4 + step] if step >= MB else []

        assert sum(len(first_unit_chunks(i)) for i in range(MB + VH)) == WCH - 2 * K

        FIRST_ORDER = [(0, 0), (1, 0)]
        for o in range(K - 2):
            FIRST_ORDER += [(o, 1), (o + 2, 0)]
        FIRST_ORDER += [(K - 2, 1), (K - 1, 1)]

        def m_block(first, j):
            if not first:
                return j // 2, j % 2, ps_w[j % 4], j + 1
            o, side = FIRST_ORDER[j]
            return o, side, (ps_w + ps_c)[o] if side == 0 else ps_w[o % 2], K * side + o + 1

        def m_read(first, o, side):
            return FIRST_ORDER.index((o, side)) + 1 if first else 2 * o + side + 1

        block = ctx.enter_context(nc.Block())

        @block.sync
        def _(sp):
            def load_stat_rows(g, q):
                if q == 0:
                    wait(sp, s_x_lo, K * g)
                else:
                    wait(sp, s_x_mv, 4 * g + q)
                sp.dma_start(stat_rows[:], x[bass.ds(g * ROWS + q * P, P), :]).then_inc(s_stat_in, 16)

            def load_xt(g, k):
                if k != 0:
                    wait(sp, s_x_lo, K * g + k - 1)
                sp.dma_start(xt_in[k % 2][:], xt[k * P:(k + 1) * P, bass.ds(g * ROWS, ROWS)]
                             ).then_inc(s_xt_in[k % 2], 16)

            def spread_stats(g):
                wait(sp, s_x_stat, g * 2 + 2)
                with nc.allow_non_contiguous_dma(reason="8 statistics for each partition"):
                    for w in range(2):
                        sp.dma_start(scratch[bass.ds(g, 1), w, :].rearrange("o (q p) -> p (o q)", p=P),
                                     x_stat[:, w, :]).then_inc(s_bc_out, 16)
                wait(sp, s_bc_out, g * 32 + 32)
                wait(sp, s_x_mul, K * g)
                sp.dma_start(bc_stats[:], scratch[bass.ds(g, 1), :, :].rearrange("o w r -> o (w r)")
                             .broadcast_to([P, 2 * ROWS])).then_inc(s_bc_in, 16)

            def load_res(G, p):
                wait(sp, s_out[p % 2], 32 * G + 16 * (p // 2))
                sp.dma_start(res_rows[p % 2][:], x[bass.ds(G * ROWS + p * P, P), :]).then_inc(s_res_in[p % 2], 16)

            def store(G, p):
                wait(sp, s_f, 4 * G + p + 1)
                sp.dma_start(out[bass.ds(G * ROWS + p * P, P), :], res_rows[p % 2][:]).then_inc(s_out[p % 2], 16)

            def load_adj(pos, it):
                n = 4 * it + pos
                g = 2 * it + pos % 2
                wait(sp, s_um, n)
                sp.dma_start(mask[0:S, :, :], adjt[bass.ds(g * GG, GG), :, :].rearrange("g j i -> j g i")
                             ).then_inc(s_adj_in, 16)
                sp.dma_start(mask[S:P, :, :], adj[bass.ds(g * GG, GG), :, :].rearrange("g j i -> j g i")
                             ).then_inc(s_adj_in, 16)
                wait(sp, s_e, 2 * n)
                of_pair = adjt[bass.ds(g * GG, GG), :, :].rearrange("(p s) j i -> s j p i", s=2)
                for s in range(2):
                    sp.dma_start(adj_e[s * S:(s + 1) * S, :, :], of_pair[s]).then_inc(s_adje_in, 16)

            def unit(pos, it):
                load_adj(pos, it)
                fin, pre = finals(pos, it), prepares(pos, it)
                G, g = final_group(pos, it), prepared_group(pos, it)
                if pre:
                    load_stat_rows(g, 0)
                    load_xt(g, 0)
                    load_xt(g, 1)
                if fin:
                    if pos == 3:
                        wait(sp, s_w_lo, WCH)
                    load_res(G, 0)
                    load_res(G, 1)
                if pre:
                    for q in range(1, PAIRS):
                        load_stat_rows(g, q)
                    spread_stats(g)
                if fin:
                    store(G, 0)
                    load_res(G, 2)
                    store(G, 1)
                    load_res(G, 3)
                    store(G, 2)
                if pre:
                    for k in range(2, K - 1):
                        load_xt(g, k)
                if fin:
                    store(G, 3)
                if pre:
                    load_xt(g, K - 1)

            for q in range(PAIRS):
                sp.dma_start(x_stage[q], x[q * P:(q + 1) * P, :]).then_inc(s_x0_in[q], 16)
            load_xt(0, 0)
            load_xt(0, 1)
            spread_stats(0)
            for k in range(2, K):
                load_xt(0, k)
            for l in range(2):
                sp.dma_start(b_lin_bc[l][:], b_lin[l:l + 1, :].broadcast_to([P, H])).then_inc(s_const, 16)
            sp.dma_start(a_bc[:], ln_a[1:2, :].broadcast_to([P, H])).then_inc(s_const, 16)
            sp.dma_start(b_bc[:], ln_b[1:2, :].broadcast_to([P, H])).then_inc(s_const, 16)
            with nc.allow_non_contiguous_dma(reason="one layer norm vector down the partitions"):
                sp.dma_start(a_col[:], ln_a[0, :].rearrange("(k p) -> p k", p=P)).then_inc(s_const, 16)
                sp.dma_start(b_col[:], ln_b[0, :].rearrange("(k p) -> p k", p=P)).then_inc(s_const, 16)
            all_units(sp, unit)
            G = NGROUP - 1
            load_res(G, 0)
            load_res(G, 1)
            for p in range(PAIRS):
                store(G, p)
                if p + 2 < PAIRS:
                    load_res(G, p + 2)
            for i in range(2):
                wait(sp, s_out[i], 32 * NGROUP)
            wait(sp, s_bc_out, 32 * NGROUP)

        @block.gpsimd
        def _(pool):
            steps = [0]

            def finish(ins):
                steps[0] += 1
                ins.then_inc(s_setup, 1)
                pool.wait_ge(s_setup, steps[0])

            finish(nc.gpsimd.memset(half_pow[:], 0.5))
            finish(nc.gpsimd.memset(neg_half_pow[:], -0.5))
            finish(nc.gpsimd.memset(tri[:], 1.0))
            finish(nc.gpsimd.memset(ident[:], 0.0))
            finish(nc.gpsimd.affine_select(out=ident[:], in_=ident[:], compare_op=ALU.not_equal, fill=1.0,
                                           base=0, pattern=[[-1, P]], channel_multiplier=1))
            finish(nc.gpsimd.affine_select(out=tri[0:S, :], in_=tri[0:S, :], compare_op=ALU.is_ge, fill=0.0,
                                           base=0, pattern=[[-1, S]], channel_multiplier=1))
            finish(nc.gpsimd.affine_select(out=tri[S:P, :], in_=tri[S:P, :], compare_op=ALU.is_gt, fill=0.0,
                                           base=0, pattern=[[1, S]], channel_multiplier=-1))
            finish(nc.gpsimd.memset(block_ones[:], 0.0))
            finish(nc.gpsimd.memset(block_ones[0:S, 0:S], 1.0))
            finish(nc.gpsimd.memset(block_ones[S:P, S:P], 1.0))
            for c in range(WSLOT):
                load_weights(pool, c)

            def x_stats(g):
                wait(pool, s_bc_out, 32 * g)
                pool.wait_ge(s_x_var, g + 1)
                nc.gpsimd.tensor_tensor(x_stat[:, 1, :], x_var[:], neg_half_pow[:], ALU.pow).then_inc(s_x_stat, 1)
                nc.gpsimd.tensor_copy(x_stat[:, 0, :], x_mv[:, :, 0]).then_inc(s_x_stat, 1)

            def context_stats(c, p):
                pool.wait_ge(s_c_mv, c + 1)
                nc.gpsimd.tensor_tensor(c_sd[:, p:p + 1], c_mv[:, p, 1:2], half_pow[:], ALU.pow).then_inc(s_c_sd, 1)

            def unit(pos, it):
                n = 4 * it + pos
                pool.wait_ge(s_adj_in, 32 * n + 32)
                nc.gpsimd.tensor_tensor(mask[:], mask[:], tri[:].unsqueeze(1).broadcast_to([P, GG, S]),
                                        ALU.mult).then_inc(s_mask, 1)
                if not has_context(pos, it):
                    for c in range(2 * K, WCH):
                        load_weights(pool, c)
                        if c == 2 * K + 9:
                            x_stats(prepared_group(pos, it))
                    return
                for j in range(0, MB, 2):
                    if j < 2 * PAIRS:
                        context_stats(4 * (n - 1) + j // 2, j // 2)
                    if j == 2 and prepares(pos, it):
                        x_stats(prepared_group(pos, it))

            x_stats(0)
            for c in range(WSLOT, 2 * K):
                load_weights(pool, c)
            all_units(pool, unit)
            for p in range(PAIRS):
                context_stats(4 * (4 * ITER - 1) + p, p)

        @block.scalar
        def _(act):
            def split_weights(c):
                m, k = c // K, c % K
                act.wait_ge(s_w[w_slot[c]], 16 * w_turn[c])
                nc.scalar.activation(w_hi[m][:, k, :], w_stage[w_slot[c]], ACT.Copy, scale=W_SCALE
                                     ).then_inc(s_w_hi, 1)

            def x_hi(g, k, buf):
                act.wait_ge(s_x_mul, K * g + k + 1)
                nc.scalar.activation(ht_hi[buf][:, k, :], xt_in[k % 2][:], ACT.Relu).then_inc(s_x_hi, 1)

            def norm(c, p, slot_wait=None, banks=ps_c):
                act.wait_ge(s_c_bias, c + 1)
                if slot_wait is not None:
                    act.wait_ge(*slot_wait)
                for i in range(2):
                    ins = nc.scalar.activation(norm_rows[p % 2][:, i * HALF:(i + 1) * HALF], banks[i][:, 0:HALF],
                                               ACT.Identity, scale=c_scale[:, p:p + 1], bias=c_bias[:, p:p + 1])
                ins.then_inc(s_norm, 1)

            def last_norm(p):
                norm(4 * (4 * ITER - 1) + p, p, (s_f, 4 * (NGROUP - 1) + p - 1), last_banks(p))

            def prepare(pos, it, step):
                k = step - X_STEP
                if prepares(pos, it) and 0 <= k < K:
                    if k == 0:
                        wait(act, s_v, VH * (4 * it + pos))
                    x_hi(prepared_group(pos, it), k, (pos + 1) % 2)

            def unit(pos, it):
                n = 4 * it + pos
                t0 = t_before(pos, it)
                first = isinstance(it, int) and n == 0
                for j in range(MB):
                    o, side, bank, ended = m_block(first, j)
                    act.wait_ge(s_m, MB * n + ended)
                    if side == 0:
                        wait(act, s_s, K * n + o - 1)
                    nc.scalar.activation(mt_hi[o % 2][:, :, side, :],
                                         bank[:].rearrange("f (g r) -> f g r", r=S), ACT.Copy,
                                         scale=1.0 / W_SCALE).then_inc(s_m_hi, 1)
                    if transposes(pos) and 3 <= j < 3 + TS:
                        t = j - 3
                        act.wait_ge(s_t, t0 + t + 1)
                        if t >= 2:
                            act.wait_ge(s_t_lo, t0 + t - 1)
                        for i in range(3):
                            k = 3 * (t % 2) + i
                            ins = nc.scalar.activation(t_relu[t % 2][:, i * P:(i + 1) * P], ps_x[:, i * P:(i + 1) * P],
                                                       ACT.Relu, scale=a_col[:, k:k + 1], bias=b_col[:, k:k + 1])
                        ins.then_inc(s_t_relu, 1)
                    if has_context(pos, it) and j in (2, 4, 6, 8):
                        p = j // 2 - 1
                        if transposes(pos):
                            free = (s_t, t0 + 2 * (p - 1)) if p >= 2 else (s_w_lo, WCH)
                        else:
                            G = final_group(pos, it)
                            free = (s_f, 4 * G + p - 1) if p >= 2 or pos == 0 else None
                        norm(4 * (n - 1) + p, p, free)
                    prepare(pos, it, j)
                    if first:
                        for c in first_unit_chunks(j):
                            split_weights(c)
                for h in range(VH):
                    act.wait_ge(s_v_sum, VH * n + h + 1)
                    if h == 0:
                        wait(act, s_av, 4 * n)
                    nc.scalar.activation(v_hi[:, h // 2, (h % 2) * HALF:(h % 2 + 1) * HALF], v_sum[h % 2][:],
                                         ACT.Copy).then_inc(s_v_hi, 1)
                    if h == 0:
                        act.wait_ge(s_um, n + 1)
                        nc.scalar.copy(u_shift[0:S, :, :], um[S:P, 0::2, :]).then_inc(s_shift, 1)
                        nc.scalar.copy(u_shift[S:P, :, :], um[0:S, 1::2, :]).then_inc(s_shift, 1)
                        act.wait_ge(s_u, 2 * n + 2)
                        nc.scalar.activation(e_t[:], u_shift[:], ACT.Exp, scale=TEMPER_INV).then_inc(s_exp, 1)
                    prepare(pos, it, MB + h)
                    if first:
                        for c in first_unit_chunks(MB + h):
                            split_weights(c)
                    if is_last(pos, it) and h == VH - 1:
                        last_norm(0)

            split_weights(0)
            split_weights(1)
            for k in range(K):
                x_hi(0, k, 0)
                split_weights(k + 2)
            for c in range(K + 2, 2 * K):
                split_weights(c)
            act.wait_ge(s_const, 6 * 16)
            all_units(act, unit)
            for p in range(1, PAIRS):
                last_norm(p)

        @block.vector
        def _(dve):
            def carry_wait():
                nc.vector.memset(carrier[:], 0.0)

            def split_weights(c):
                m, k = c // K, c % K
                dve.wait_ge(s_w_hi, c + 1)
                nc.vector.scalar_tensor_tensor(w_lo[m][:, k, :], w_stage[w_slot[c]], W_SCALE, w_hi[m][:, k, :],
                                               ALU.mult, ALU.subtract).then_inc(s_w_lo, 1)

            def x_row_stats(g, q):
                if isinstance(g, int) and g == 0:
                    rows = x_stage[q]
                    dve.wait_ge(s_x0_in[q], 16)
                else:
                    rows = stat_rows[:]
                    dve.wait_ge(s_stat_in, 64 * g + 16 * q - 48)
                for i in range(2):
                    nc.vector.bn_stats(x_bn[:, q, i, :], rows[:, i * HALF:(i + 1) * HALF]).then_inc(s_x_bn, 1)
                if q == 0:
                    wait(dve, s_x_stat, 2 * g)
                dve.wait_ge(s_x_bn, 8 * g + 2 * q + 2)
                carry_wait()
                nc.vector.bn_aggr(x_mv[:, q, :], x_bn[:, q, :, :].rearrange("p a b -> p (a b)")).then_inc(s_x_mv, 1)
                if q == PAIRS - 1:
                    dve.wait_ge(s_x_mv, 4 * g + 4)
                    nc.vector.tensor_scalar(x_var[:], x_mv[:, :, 1], LN_X_EPS, None, ALU.add).then_inc(s_x_var, 1)

            def x_norm(g, k):
                dve.wait_ge(s_xt_in[k % 2], 48 * g + 16 * (k // 2) + 16)
                if k == 0:
                    dve.wait_ge(s_bc_in, 16 * g + 16)
                nc.vector.tensor_tensor(xt_in[k % 2][:], xt_in[k % 2][:], bc_stats[:, 0, :], ALU.subtract
                                        ).then_inc(s_x_sub, 1)
                dve.wait_ge(s_x_sub, K * g + k + 1)
                nc.vector.tensor_tensor(xt_in[k % 2][:], xt_in[k % 2][:], bc_stats[:, 1, :], ALU.mult
                                        ).then_inc(s_x_mul, 1)

            def x_lo(g, k, buf):
                dve.wait_ge(s_x_hi, K * g + k + 1)
                nc.vector.scalar_tensor_tensor(ht_lo[buf][:, k, :], xt_in[k % 2][:], 0.0, ht_hi[buf][:, k, :],
                                               ALU.max, ALU.subtract).then_inc(s_x_lo, 1)

            def context_stats(c, p, banks=ps_c):
                dve.wait_ge(s_av, c + 1)
                for i in range(2):
                    nc.vector.bn_stats(c_bn[:, p, i, :], banks[i][:, 0:HALF]).then_inc(s_c_bn, 1)
                dve.wait_ge(s_c_bn, 2 * c + 2)
                carry_wait()
                nc.vector.bn_aggr(c_mv[:, p, :], c_bn[:, p, :, :].rearrange("p a b -> p (a b)")).then_inc(s_c_mv, 1)

            def context_scale(c, p):
                dve.wait_ge(s_c_sd, c + 1)
                nc.vector.tensor_scalar(c_den[:, p:p + 1], c_sd[:, p:p + 1], STD_FIX, LN_EPS * ATT_SCALE,
                                        ALU.mult, ALU.add).then_inc(s_c_den, 1)
                dve.wait_ge(s_c_den, c + 1)
                nc.vector.reciprocal(c_scale[:, p:p + 1], c_den[:, p:p + 1]).then_inc(s_c_scale, 1)
                dve.wait_ge(s_c_scale, c + 1)
                nc.vector.scalar_tensor_tensor(c_bias[:, p:p + 1], c_mv[:, p, 0:1], -1.0, c_scale[:, p:p + 1],
                                               ALU.mult, ALU.mult).then_inc(s_c_bias, 1)

            def final(c, G, p):
                rows, res = norm_rows[p % 2], res_rows[p % 2]
                dve.wait_ge(s_norm, c + 1)
                nc.vector.tensor_tensor(rows[:], rows[:], a_bc[:], ALU.mult).then_inc(s_fa, 1)
                dve.wait_ge(s_fa, 4 * G + p + 1)
                nc.vector.tensor_tensor(rows[:], rows[:], b_bc[:], ALU.add).then_inc(s_fb, 1)
                dve.wait_ge(s_fb, 4 * G + p + 1)
                dve.wait_ge(s_res_in[p % 2], 32 * G + 16 * (p // 2) + 16)
                nc.vector.scalar_tensor_tensor(res[:], rows[:], 0.0, res[:], ALU.max, ALU.add).then_inc(s_f, 1)

            def v_lo_part(n, h):
                dve.wait_ge(s_v_hi, VH * n + h + 1)
                at = slice((h % 2) * HALF, (h % 2 + 1) * HALF)
                nc.vector.tensor_tensor(v_lo[:, h // 2, at], v_sum[h % 2][:], v_hi[:, h // 2, at], ALU.subtract
                                        ).then_inc(s_v_lo, 1)

            LAST = 4 * (4 * ITER - 1)

            def last_stats(p):
                context_stats(LAST + p, p, last_banks(p))
                context_scale(LAST + p, p)

            def prepare(pos, it, step):
                k = step - X_STEP
                if prepares(pos, it):
                    if 1 <= k <= K:
                        x_lo(prepared_group(pos, it), k - 1, (pos + 1) % 2)
                    if 0 <= k < K:
                        x_norm(prepared_group(pos, it), k)

            def unit(pos, it):
                n = 4 * it + pos
                t0 = t_before(pos, it)
                layer = pos // 2
                first = isinstance(it, int) and n == 0
                for j in range(MB):
                    o, side, bank, _ = m_block(first, j)
                    dve.wait_ge(s_m_hi, MB * n + j + 1)
                    nc.vector.scalar_tensor_tensor(mt_lo[o % 2][:, :, side, :],
                                                   bank[:].rearrange("f (g r) -> f g r", r=S),
                                                   1.0 / W_SCALE,
                                                   mt_hi[o % 2][:, :, side, :], ALU.mult, ALU.subtract
                                                   ).then_inc(s_m_lo, 1)
                    if has_context(pos, it) and j in (2, 4, 6, 8):
                        context_scale(4 * (n - 1) + j // 2 - 1, j // 2 - 1)
                    if has_context(pos, it) and j in (1, 3, 5, 7):
                        context_stats(4 * (n - 1) + j // 2, j // 2)
                    if transposes(pos) and 3 <= j < 3 + TS:
                        t = j - 3
                        dve.wait_ge(s_t_relu, t0 + t + 1)
                        if t == 0:
                            wait(dve, s_v, VH * n)
                        to = (slice(None), slice(3 * (t % 2), 3 * (t % 2) + 3), slice(t // 2 * P, (t // 2 + 1) * P))
                        part = t_relu[t % 2][:].rearrange("f (k r) -> f k r", r=P)
                        buf = (pos + 1) % 2
                        nc.vector.tensor_copy(ht_hi[buf][to], part).then_inc(s_t_hi, 1)
                        dve.wait_ge(s_t_hi, t0 + t + 1)
                        nc.vector.tensor_tensor(ht_lo[buf][to], part, ht_hi[buf][to], ALU.subtract
                                                ).then_inc(s_t_lo, 1)
                    if finals(pos, it) and j in (3, 5, 7, 9):
                        p = (j - 3) // 2
                        final(4 * (n - 1) + p, final_group(pos, it), p)
                    if prepares(pos, it) and j < PAIRS:
                        x_row_stats(prepared_group(pos, it), j)
                    prepare(pos, it, j)
                    if first:
                        for c in first_unit_chunks(j):
                            split_weights(c)
                for h in range(VH):
                    if h >= 1:
                        v_lo_part(n, h - 1)
                    dve.wait_ge(s_v, VH * n + h + 1)
                    nc.vector.scalar_tensor_tensor(v_sum[h % 2][:], ps_w[h % 4][:, 0:HALF], 1.0 / W_SCALE,
                                                   b_lin_bc[layer][:, (h % 2) * HALF:(h % 2 + 1) * HALF],
                                                   ALU.mult, ALU.add).then_inc(s_v_sum, 1)
                    if h == 0:
                        dve.wait_ge(s_s, K * n + K)
                        dve.wait_ge(s_mask, n + 1)
                        nc.vector.tensor_tensor(um[:], ps_s[:], mask[:], ALU.mult).then_inc(s_um, 1)
                        for s in range(2):
                            at = slice(s * S, (s + 1) * S)
                            dve.wait_ge(s_shift, 2 * n + 1 + s)
                            nc.vector.tensor_tensor(u_shift[at, :, :], um[at, s::2, :], u_shift[at, :, :], ALU.add
                                                    ).then_inc(s_u, 1)
                    if h == 1:
                        dve.wait_ge(s_exp, n + 1)
                        dve.wait_ge(s_adje_in, 32 * n + 32)
                        nc.vector.tensor_tensor(e_t[:], e_t[:], adj_e[:], ALU.mult).then_inc(s_e, 2)
                    if h == 4:
                        dve.wait_ge(s_den, n + 1)
                        nc.vector.tensor_scalar(den[:], ps_x[:, 0:PAIRS * S].rearrange("p (a b) -> p a b", b=S),
                                                DEN_EPS, None, ALU.add).then_inc(s_den_rd, 1)
                        dve.wait_ge(s_den_rd, n + 1)
                        nc.vector.reciprocal(den[:], den[:]).then_inc(s_recip, 1)
                        dve.wait_ge(s_recip, n + 1)
                        nc.vector.scalar_tensor_tensor(e_t[:], e_t[:], ATT_SCALE, den[:], ALU.mult, ALU.mult
                                                       ).then_inc(s_att, 1)
                        dve.wait_ge(s_att, n + 1)
                        for s in range(2):
                            at = slice(s * S, (s + 1) * S)
                            nc.vector.tensor_copy(att_hi[at, :, at], e_t[at, :, :]).then_inc(s_att_hi, 1)
                        for s in range(2):
                            at = slice(s * S, (s + 1) * S)
                            dve.wait_ge(s_att_hi, 2 * n + 1 + s)
                            nc.vector.tensor_tensor(att_lo[at, :, at], e_t[at, :, :], att_hi[at, :, at],
                                                    ALU.subtract).then_inc(s_att_lo, 1)
                    prepare(pos, it, MB + h)
                    if first:
                        for c in first_unit_chunks(MB + h):
                            split_weights(c)
                    if is_last(pos, it) and h == VH - 1:
                        last_stats(0)
                v_lo_part(n, VH - 1)

            nc.vector.memset(att_hi[:], 0.0).then_inc(s_clear, 1)
            nc.vector.memset(att_lo[:], 0.0).then_inc(s_clear, 1)
            dve.wait_ge(s_clear, 2)
            for q in range(PAIRS):
                x_row_stats(0, q)
            split_weights(0)
            split_weights(1)
            for k in range(K):
                x_norm(0, k)
                split_weights(k + 2)
                x_lo(0, k, 0)
            for c in range(K + 2, 2 * K):
                split_weights(c)
            dve.wait_ge(s_const, 6 * 16)
            all_units(dve, unit)
            for p in range(1, PAIRS):
                last_stats(p)
                final(LAST + p - 1, NGROUP - 1, p - 1)
            final(LAST + PAIRS - 1, NGROUP - 1, PAIRS - 1)

        @block.tensor
        def _(pe):
            def three_passes(ps, pieces, sem, weights_moving=False):
                last = len(pieces) - 1
                for i, (st_hi, st_lo, mv_hi, mv_lo) in enumerate(pieces):
                    nc.tensor.matmul(ps, st_hi, mv_hi, start=(i == 0), stop=False)
                    nc.tensor.matmul(ps, st_hi, mv_lo, start=False, stop=False)
                    ins = nc.tensor.matmul(ps, st_lo, mv_hi, start=False, stop=(i == last))
                if sem is not None:
                    ins.then_inc(sem, 1)

            def scores(n, buf, o, first):
                pe.wait_ge(s_m_lo, MB * n + m_read(first, o, 1))
                if o == 0:
                    wait(pe, s_um, n)
                for q in range(GG):
                    at = slice(q * S, (q + 1) * S)
                    m_hi = mt_hi[o % 2][:, q, :, :].rearrange("f s r -> f (s r)")
                    m_lo = mt_lo[o % 2][:, q, :, :].rearrange("f s r -> f (s r)")
                    for i, (m, h) in enumerate(((m_hi, ht_hi), (m_hi, ht_lo), (m_lo, ht_hi))):
                        ins = nc.tensor.matmul(ps_s[:, q, :], m, h[buf][:, o, at],
                                               start=(o == 0 and q == 0 and i == 0), stop=(o == K - 1 and i == 2),
                                               skip_group_check=True)
                ins.then_inc(s_s, 1)

            def context_of(p, banks):
                for i in range(2):
                    at = slice(i * HALF, (i + 1) * HALF)
                    three_passes(banks[i][:, 0:HALF],
                                 [(att_hi[:, p, :], att_lo[:, p, :], v_hi[:, p, at], v_lo[:, p, at])],
                                 s_av if i == 1 else None)

            def context(c, p, n):
                if p == 0:
                    pe.wait_ge(s_att_lo, 2 * n)
                    pe.wait_ge(s_v_lo, VH * n)
                wait(pe, s_norm, c)
                context_of(p, ps_c)

            def last_context(p):
                n = 4 * ITER - 1
                if p == 0:
                    pe.wait_ge(s_att_lo, 2 * n + 2)
                pe.wait_ge(s_v_lo, VH * n + 2 * (p + 1))
                pe.wait_ge(s_norm, PAIRS * n + max(p - 1, 0))
                context_of(p, last_banks(p))

            def unit(pos, it):
                n = 4 * it + pos
                buf = pos % 2
                layer = pos // 2
                t0 = t_before(pos, it)
                first = isinstance(it, int) and n == 0
                hh, hl = ht_hi[buf], ht_lo[buf]
                if first:
                    for k in range(K):
                        pe.wait_ge(s_x_lo, k + 1)
                        pe.wait_ge(s_w_lo, k + 1)
                        for o in range(K):
                            of = slice(o * P, (o + 1) * P)
                            bank = (ps_w + ps_c)[o][:]
                            nc.tensor.matmul(bank, w_hi[0][:, k, of], hh[:, k, :], start=(k == 0), stop=False)
                            nc.tensor.matmul(bank, w_hi[0][:, k, of], hl[:, k, :], start=False, stop=False)
                            ins = nc.tensor.matmul(bank, w_lo[0][:, k, of], hh[:, k, :], start=False,
                                                   stop=(k == K - 1))
                            if k == K - 1:
                                ins.then_inc(s_m, 1)
                    pe.wait_ge(s_w_lo, 2 * K)
                elif layer == 0:
                    pe.wait_ge(s_x_lo, K * (2 * it + pos) + K)
                else:
                    pe.wait_ge(s_t_lo, 16 * it + (8 if pos == 2 else 16))
                    pe.wait_ge(s_w_lo, WCH)
                for j in range(MB):
                    o, side = j // 2, j % 2
                    m = 3 * layer + side
                    bank = ps_w[o % 2] if first else ps_w[j % 4]
                    if first:
                        if side == 0:
                            continue
                        pe.wait_ge(s_m_lo, m_read(True, o, 0) if o < 2 else m_read(True, o - 2, 1))
                    elif j < 4:
                        wait(pe, s_v_sum, VH * n - 3 + j)
                    else:
                        pe.wait_ge(s_m_lo, MB * n + j - 3)
                    three_passes(bank[:],
                                 [(w_hi[m][:, k, o * P:(o + 1) * P], w_lo[m][:, k, o * P:(o + 1) * P],
                                   hh[:, k, :], hl[:, k, :]) for k in range(K)], s_m)
                    if side == 1 and o >= 1:
                        scores(n, buf, o - 1, first)
                    if has_context(pos, it) and j in (1, 3, 5, 7):
                        context(4 * (n - 1) + j // 2, j // 2, n)
                    if transposes(pos) and 3 <= j < 3 + TS:
                        t = j - 3
                        if t % 2 == 0:
                            pe.wait_ge(s_norm, 4 * (n - 1) + t // 2 + 1)
                        if t == 0:
                            pe.wait_ge(s_den_rd, n)
                        else:
                            pe.wait_ge(s_t_relu, t0 + t)
                        for i in range(3):
                            k = 3 * (t % 2) + i
                            ins = nc.tensor.transpose(ps_x[:, i * P:(i + 1) * P],
                                                      norm_rows[(t // 2) % 2][:, k * P:(k + 1) * P], ident[:])
                        ins.then_inc(s_t, 1)
                if first:
                    pe.wait_ge(s_w_lo, 3 * K)
                for h in range(VH):
                    if h < 4:
                        pe.wait_ge(s_m_lo, MB if first else MB * n + MB - 3 + h)
                    else:
                        pe.wait_ge(s_v_sum, VH * n + h - 3)
                    m = 3 * layer + 2
                    rows = slice(h // 2 * P, (h // 2 + 1) * P)
                    cols = slice((h % 2) * HALF, (h % 2 + 1) * HALF)
                    three_passes(ps_w[h % 4][:, 0:HALF],
                                 [(hh[:, k, rows], hl[:, k, rows], w_hi[m][:, k, cols], w_lo[m][:, k, cols])
                                  for k in range(K)], s_v)
                    if h == 0:
                        scores(n, buf, K - 1, first)
                    if h == 3:
                        pe.wait_ge(s_e, 2 * n + 2)
                        if transposes(pos):
                            pe.wait_ge(s_t_relu, t0 + TS)
                        else:
                            wait(pe, s_den_rd, n)
                        nc.tensor.matmul(ps_x[:, 0:PAIRS * S], block_ones[:], e_t[:].rearrange("p a b -> p (a b)"),
                                         start=True, stop=True).then_inc(s_den, 1)
                    if is_last(pos, it) and h >= VH - 2:
                        last_context(h - 6)

            pe.wait_ge(s_setup, 10)
            pe.wait_ge(s_clear, 2)
            all_units(pe, unit)
            last_context(2)
            last_context(3)


def kernel(**inputs):
    import numpy as np
    import concourse.bacc as bacc
    from concourse.bass_utils import run_bass_kernel_spmd

    x = np.asarray(inputs["x"])
    adj = np.asarray(inputs["adj"])
    B, S, H = x.shape
    rows = np.ascontiguousarray(x.reshape(B * S, H))
    wt = np.stack([np.asarray(inputs[f"L0_gnn_{n}"]) for n in ("W_left", "W_right", "W_lin")], axis=1)
    wt = np.ascontiguousarray(wt.transpose(0, 1, 3, 2).reshape(-1, H, H))
    arrays = {
        "x_rows": rows,
        "x_cols": np.ascontiguousarray(rows.T),
        "adj": np.ascontiguousarray(adj),
        "adj_t": np.ascontiguousarray(adj.transpose(0, 2, 1)),
        "w_t": wt,
        "b_lin": np.ascontiguousarray(inputs["L0_gnn_b_lin"]),
        "ln_a": np.ascontiguousarray(inputs["L0_gnn_ln_a"]),
        "ln_b": np.ascontiguousarray(inputs["L0_gnn_ln_b"]),
    }
    nc = bacc.Bacc("TRN2", target_bir_lowering=False, num_devices=1)
    aps = [nc.dram_tensor(n, a.shape, mybir.dt.from_np(a.dtype), kind="ExternalInput").ap() for n, a in arrays.items()]
    out = nc.dram_tensor("out", (B * S, H), F32, kind="ExternalOutput").ap()
    build(nc, *aps, out)
    r = run_bass_kernel_spmd(nc, [arrays], core_ids=[0])
    return r.results[0]["out"].reshape(B, S, H)
```

```python
from contextlib import ExitStack

import concourse.bass as bass
from concourse import mybir

P = 128
F32 = mybir.dt.float32
F16 = mybir.dt.float16
ALU = mybir.AluOpType
ACT = mybir.ActivationFunctionType

W_SCALE = 2.0 ** 6
ATT_SCALE = 2.0 ** 11
LN_X_EPS = 1e-5
LN_EPS = 1e-3
DEN_EPS = 1e-10


def wait(eng, sem, count):
    if isinstance(count, int) and count <= 0:
        return
    eng.wait_ge(sem, count)


def build(nc, x, adj, adjt, wt, b_lin, ln_a, ln_b, out):
    GRAPHS, S, _ = adj.shape
    H = x.shape[1]
    K = H // P
    HALF = H // 2
    PAIRS = 4
    ROWS = PAIRS * P
    GG = 2 * PAIRS
    NGROUP = GRAPHS // GG
    ITER = NGROUP // 2
    TEMPER_INV = 1.0 / float(H) ** 0.5
    STD_FIX = (H / (H - 1.0)) ** 0.5
    MB = 2 * K
    VH = 2 * PAIRS
    WCH = 6 * K
    WSLOT = 4

    with ExitStack() as ctx:
        def sb(name, shape, dt=F32):
            return ctx.enter_context(nc.sbuf_tensor(name, shape, dt))

        def sem(name):
            return ctx.enter_context(nc.semaphore(name))

        w_hi = [sb(f"w_hi{m}", [P, K, H], F16) for m in range(6)]
        w_lo = [sb(f"w_lo{m}", [P, K, H], F16) for m in range(6)]
        ht_hi = [sb(f"ht_hi{i}", [P, K, ROWS], F16) for i in range(2)]
        ht_lo = [sb(f"ht_lo{i}", [P, K, ROWS], F16) for i in range(2)]
        mt_hi = [sb(f"mt_hi{i}", [P, GG, 2, S], F16) for i in range(2)]
        mt_lo = [sb(f"mt_lo{i}", [P, GG, 2, S], F16) for i in range(2)]
        v_hi = sb("v_hi", [P, PAIRS, H], F16)
        v_lo = sb("v_lo", [P, PAIRS, H], F16)
        att_hi = sb("att_hi", [P, PAIRS, P], F16)
        att_lo = sb("att_lo", [P, PAIRS, P], F16)
        norm_rows = [sb(f"norm_rows{i}", [P, H]) for i in range(2)]
        res_rows = [sb(f"res_rows{i}", [P, H]) for i in range(2)]
        x_in = [sb(f"x_in{i}", [P, H]) for i in range(2)]
        h_hi = [sb(f"h_hi{i}", [P, H], F16) for i in range(2)]
        h_lo = [sb(f"h_lo{i}", [P, H], F16) for i in range(2)]
        b_lin_bc = [sb(f"b_lin_bc{l}", [P, H]) for l in range(2)]
        a_bc = [sb(f"a_bc{l}", [P, H]) for l in range(2)]
        b_bc = [sb(f"b_bc{l}", [P, H]) for l in range(2)]
        v_sum = [sb(f"v_sum{i}", [P, HALF]) for i in range(2)]
        mask = sb("mask", [P, GG, S])
        adj_e = sb("adj_e", [P, PAIRS, S])
        um = sb("um", [P, GG, S])
        u_shift = sb("u_shift", [P, PAIRS, S])
        den = u_shift
        e_t = sb("e_t", [P, PAIRS, S])
        tri = sb("tri", [P, S])
        block_ones = sb("block_ones", [P, P])
        half_pow = sb("half_pow", [P, 1])
        neg_half_pow = sb("neg_half_pow", [P, 1])
        x_bn = sb("x_bn", [P, PAIRS, 2, 6])
        x_mv = sb("x_mv", [P, PAIRS, 2])
        x_var = sb("x_var", [P, PAIRS])
        x_scale = sb("x_scale", [P, PAIRS])
        x_bias = sb("x_bias", [P, PAIRS])
        c_bn = sb("c_bn", [P, PAIRS, 2, 6])
        c_mv = sb("c_mv", [P, PAIRS, 2])
        c_sd = sb("c_sd", [P, PAIRS])
        c_den = sb("c_den", [P, PAIRS])
        c_scale = sb("c_scale", [P, PAIRS])
        carrier = sb("carrier", [P, 1])
        c_bias = sb("c_bias", [P, PAIRS])
        first_h = [(h_hi[i][:], h_lo[i][:]) for i in range(2)]
        for t in x_in:
            halves = t[:].bitcast(F16)
            first_h.append((halves[:, 0:H], halves[:, H:2 * H]))
        halves = ht_hi[0][:].rearrange("p a h -> p (a h)").bitcast(F32)
        last_rows = [t[:] for t in norm_rows + x_in]
        last_res = [t[:] for t in res_rows] + [halves[:, 0:H], halves[:, H:2 * H]]
        w_stage = [t[:] for t in (res_rows[0], res_rows[1], norm_rows[0], norm_rows[1])]
        for t in (v_hi, v_lo):
            halves = t[:].rearrange("p a h -> p (a h)").bitcast(F32)
            w_stage += [halves[:, 0:H], halves[:, H:2 * H]]
        w_stage += [x_in[0][:], x_in[1][:]]
        x_stage = []
        for t in (ht_hi[1], ht_lo[1]):
            halves = t[:].rearrange("p a h -> p (a h)").bitcast(F32)
            x_stage += [halves[:, 0:H], halves[:, H:2 * H]]

        ps_w = [ctx.enter_context(nc.psum_tensor(f"ps_w{i}", [P, 512], F32)) for i in range(4)]
        ps_s = ctx.enter_context(nc.psum_tensor("ps_s", [P, GG, S], F32))
        ps_s_flat = ps_s[:].rearrange("p g r -> p (g r)")
        ps_x = ctx.enter_context(nc.psum_tensor("ps_x", [P, 512], F32))
        ps_c = [ctx.enter_context(nc.psum_tensor(f"ps_c{i}", [P, 512], F32)) for i in range(2)]

        s_const = sem("const_in")
        s_w = [sem(f"w_in{i}") for i in range(len(w_stage))]
        s_w_first = [sem(f"w_first_in{i}") for i in range(WSLOT)]
        s_x0_in = [sem(f"x_stage_in{i}") for i in range(PAIRS)]
        s_x_in = [sem(f"x_rows_in{i}") for i in range(2)]
        s_res_in = [sem(f"res_rows_in{i}") for i in range(2)]
        s_last_res_in = [sem(f"last_res_in{i}") for i in range(2)]
        s_out = [sem(f"out_stored{i}") for i in range(2)]
        s_adj_in = sem("adj_in")
        s_adje_in = sem("adj_e_in")
        s_setup = sem("pool_setup")
        s_clear = sem("att_cleared")
        s_w_hi = sem("w_hi_done")
        s_w_lo = sem("w_lo_done")
        s_x_bn = sem("x_bn_done")
        s_x_mv = sem("x_mv_done")
        s_x_var = sem("x_var_done")
        s_x_scale = sem("x_scale_done")
        s_x_bias = sem("x_bias_done")
        s_x_norm = sem("x_norm_done")
        s_m = sem("m_done")
        s_m_hi = sem("m_hi_done")
        s_m_lo = sem("m_lo_done")
        s_s = sem("scores_done")
        s_mask = sem("mask_done")
        s_um = sem("um_done")
        s_shift = sem("u_shift_done")
        s_u = sem("u_done")
        s_exp = sem("exp_done")
        s_e = sem("e_done")
        s_den = sem("den_done")
        s_den_rd = sem("den_read")
        s_recip = sem("recip_done")
        s_att = sem("att_done")
        s_att_hi = sem("att_hi_done")
        s_att_lo = sem("att_lo_done")
        s_v = sem("v_done")
        s_v_sum = sem("v_sum_done")
        s_v_hi = sem("v_hi_done")
        s_v_lo = sem("v_lo_done")
        s_av = sem("av_done")
        s_c_bn = sem("c_bn_done")
        s_c_mv = sem("c_mv_done")
        s_c_sd = sem("c_sd_done")
        s_c_den = sem("c_den_done")
        s_c_scale = sem("c_scale_done")
        s_c_bias = sem("c_bias_done")
        s_norm = sem("norm_done")
        s_na = sem("norm_times_a_done")
        s_nb = sem("norm_plus_b_done")
        s_h_hi = sem("h_hi_done")
        s_h_lo = sem("h_lo_done")
        s_final = sem("final_done")
        s_ht = [sem(f"ht_in{i}") for i in range(2)]
        s_ht_first = [sem(f"ht_first_in{p}") for p in range(PAIRS)]
        s_carrier = sem("sync_carrier")

        def all_units(eng, unit):
            unit(0, 0)
            unit(1, 0)
            with eng.Fori(0, ITER - 1) as i:
                unit(2, i)
                unit(3, i)
                unit(0, i + 1)
                unit(1, i + 1)
            unit(2, ITER - 1)
            unit(3, ITER - 1)

        def has_context(pos, it):
            return not (pos == 0 and isinstance(it, int) and it == 0)

        def transposes(pos):
            return pos in (1, 2)

        def finals(pos, it):
            return pos in (0, 3) and has_context(pos, it)

        def is_last(pos, it):
            return pos == 3 and isinstance(it, int) and it == ITER - 1

        def last_banks(p):
            return ((ps_c[0], ps_c[1]), (ps_s_flat, ps_x), (ps_w[0], ps_w[1]), (ps_w[2], ps_w[3]))[p]

        def final_group(pos, it):
            return 2 * it if pos == 3 else 2 * it - 1

        def prepares(pos, it):
            return pos == 0 or (pos == 3 and not (isinstance(it, int) and it == ITER - 1))

        def x_step(pos, it):
            return 6 if has_context(pos, it) else 8

        def x_turn(pos, it, step):
            return divmod(step - x_step(pos, it), 2)

        def prepared_group(pos, it):
            return 2 * it + 1 if pos == 0 else 2 * it + 2

        LAYER1_STEPS = ([(0, i) for i in (1, 2, 3, 4, 5, 14, 17, 18)]
                        + [(1, i) for i in (4, 6, 8, 10, 11, 13, 14, 15, 16, 17)])
        SECOND = 3 * K + [n for n, _ in LAYER1_STEPS].index(1)

        def chunks_at(pos, it, step):
            if not (isinstance(it, int) and it == 0):
                return []
            return [3 * K + i for i, at in enumerate(LAYER1_STEPS) if at == (pos, step)]

        w_slot = [c % (2 * WSLOT) if c < 4 * WSLOT else c % WSLOT if c < SECOND else (0, 1, 8, 9)[(c - SECOND) % 4]
                  for c in range(WCH)]
        w_before = [max([b for b in range(c) if w_slot[b] == w_slot[c]], default=-1) for c in range(WCH)]
        w_turn = [1 if c < WSLOT else w_slot[WSLOT:c + 1].count(w_slot[c]) for c in range(WCH)]
        w_in = s_w_first + [s_w[w_slot[c]] for c in range(WSLOT, WCH)]

        def load_weights(eng, c):
            if w_slot[c] >= 2 * WSLOT and w_before[c] < 0:
                eng.wait_ge(s_h_lo, 2 * PAIRS)
            wait(eng, s_w_lo, w_before[c] + 1)
            m, k = c // K, c % K
            eng.dma_start(w_stage[w_slot[c]], wt[m, k * P:(k + 1) * P, :]).then_inc(w_in[c], 16)

        FIRST_ORDER = [(0, 0), (1, 0), (0, 1), (1, 1)] + [(o, side) for o in range(2, K) for side in range(2)]

        def m_block(first, j):
            if not first:
                return j // 2, j % 2, ps_w[j % 4], j + 1
            o, side = FIRST_ORDER[j]
            return o, side, (ps_w + ps_c)[o] if side == 0 else ps_w[o % 2], K * side + o + 1

        def m_read(first, o, side):
            return FIRST_ORDER.index((o, side)) + 1 if first else 2 * o + side + 1

        block = ctx.enter_context(nc.Block())

        @block.sync
        def _(sp):
            def load_x(g, n, q):
                if isinstance(n, int) and n == 0 and q < 2:
                    sp.wait_ge(s_ht_first[q + 2], 32)
                else:
                    sp.wait_ge(s_h_lo, PAIRS * (n + 1) + max(q - 1, 0))
                sp.dma_start(x_in[q % 2][:], x[bass.ds(g * ROWS + q * P, P), :]).then_inc(s_x_in[q % 2], 16)

            def load_res(G, p):
                wait(sp, s_out[p % 2], 32 * G + 16 * (p // 2))
                sp.dma_start(res_rows[p % 2][:], x[bass.ds(G * ROWS + p * P, P), :]).then_inc(s_res_in[p % 2], 16)

            def store(G, p):
                wait(sp, s_final, PAIRS * G + p + 1)
                sp.dma_start(out[bass.ds(G * ROWS + p * P, P), :], res_rows[p % 2][:]).then_inc(s_out[p % 2], 16)

            def transpose(pos, it, p):
                n = 4 * it + pos
                sp.wait_ge(s_h_lo, PAIRS * (n + 1) + p + 1)
                sp.sem_inc(s_carrier, 1)
                if p == 0 and has_context(pos, it):
                    sp.wait_ge(s_v, VH * n)
                    sp.sem_inc(s_carrier, 1)
                for src, dst in ((h_hi, ht_hi), (h_lo, ht_lo)):
                    sp.dma_start_transpose(dst[(pos + 1) % 2][:, :, p * P:(p + 1) * P], src[p % 2][:]
                                           ).then_inc(s_ht[p % 2], 16)

            def load_adj(pos, it):
                n = 4 * it + pos
                g = 2 * it + pos % 2
                wait(sp, s_um, n)
                sp.dma_start(mask[0:S, :, :], adjt[bass.ds(g * GG, GG), :, :].rearrange("g j i -> j g i")
                             ).then_inc(s_adj_in, 16)
                sp.dma_start(mask[S:P, :, :], adj[bass.ds(g * GG, GG), :, :].rearrange("g j i -> j g i")
                             ).then_inc(s_adj_in, 16)
                wait(sp, s_e, 2 * n)
                of_pair = adjt[bass.ds(g * GG, GG), :, :].rearrange("(p s) j i -> s j p i", s=2)
                for s in range(2):
                    sp.dma_start(adj_e[s * S:(s + 1) * S, :, :], of_pair[s]).then_inc(s_adje_in, 16)

            def unit(pos, it):
                load_adj(pos, it)
                fin, pre = finals(pos, it), prepares(pos, it)
                G, g = final_group(pos, it), prepared_group(pos, it)
                n = 4 * it + pos
                if transposes(pos):
                    for p in range(PAIRS):
                        transpose(pos, it, p)
                if pos == 3:
                    wait(sp, s_w_lo, WCH)
                if pre:
                    load_x(g, n, 0)
                    load_x(g, n, 1)
                if fin:
                    load_res(G, 0)
                    load_res(G, 1)
                    store(G, 0)
                    load_res(G, 2)
                    store(G, 1)
                    load_res(G, 3)
                    store(G, 2)
                if pre:
                    transpose(pos, it, 0)
                    load_x(g, n, 2)
                if fin:
                    store(G, 3)
                if pre:
                    transpose(pos, it, 1)
                    load_x(g, n, 3)
                    transpose(pos, it, 2)
                    transpose(pos, it, 3)

            def load_first_x(q):
                sp.dma_start(x_stage[q], x[q * P:(q + 1) * P, :]).then_inc(s_x0_in[q], 16)

            load_first_x(0)
            load_first_x(1)
            for c in range(WSLOT):
                load_weights(sp, c)
            for p in range(PAIRS):
                sp.wait_ge(s_h_hi, p + 1)
                sp.dma_start_transpose(ht_hi[0][:, :, p * P:(p + 1) * P], first_h[p][0]).then_inc(s_ht_first[p], 16)
                sp.wait_ge(s_h_lo, p + 1)
                sp.dma_start_transpose(ht_lo[0][:, :, p * P:(p + 1) * P], first_h[p][1]).then_inc(s_ht_first[p], 16)
                if p == 0:
                    load_first_x(2)
                    load_first_x(3)
            sp.wait_ge(s_w_lo, 2 * K)
            for l in range(2):
                sp.dma_start(b_lin_bc[l][:], b_lin[l:l + 1, :].broadcast_to([P, H])).then_inc(s_const, 16)
                sp.dma_start(a_bc[l][:], ln_a[l:l + 1, :].broadcast_to([P, H])).then_inc(s_const, 16)
                sp.dma_start(b_bc[l][:], ln_b[l:l + 1, :].broadcast_to([P, H])).then_inc(s_const, 16)
            all_units(sp, unit)
            G = NGROUP - 1
            load_res(G, 0)
            load_res(G, 1)
            sp.wait_ge(s_v, VH * (4 * ITER - 1))
            for i in range(2):
                sp.dma_start(last_res[2 + i], x[G * ROWS + (2 + i) * P:G * ROWS + (3 + i) * P, :]
                             ).then_inc(s_last_res_in[i], 16)
            for p in range(PAIRS):
                sp.wait_ge(s_final, PAIRS * G + p + 1)
                sp.dma_start(out[G * ROWS + p * P:G * ROWS + (p + 1) * P, :], last_res[p]).then_inc(s_out[p % 2], 16)
            for i in range(2):
                wait(sp, s_out[i], 32 * NGROUP)

        @block.gpsimd
        def _(pool):
            steps = [0]

            def finish(ins):
                steps[0] += 1
                ins.then_inc(s_setup, 1)
                pool.wait_ge(s_setup, steps[0])

            finish(nc.gpsimd.memset(half_pow[:], 0.5))
            finish(nc.gpsimd.memset(neg_half_pow[:], -0.5))
            finish(nc.gpsimd.memset(tri[:], 1.0))
            finish(nc.gpsimd.affine_select(out=tri[0:S, :], in_=tri[0:S, :], compare_op=ALU.is_ge, fill=0.0,
                                           base=0, pattern=[[-1, S]], channel_multiplier=1))
            finish(nc.gpsimd.affine_select(out=tri[S:P, :], in_=tri[S:P, :], compare_op=ALU.is_gt, fill=0.0,
                                           base=0, pattern=[[1, S]], channel_multiplier=-1))
            finish(nc.gpsimd.memset(block_ones[:], 0.0))
            finish(nc.gpsimd.memset(block_ones[0:S, 0:S], 1.0))
            finish(nc.gpsimd.memset(block_ones[S:P, S:P], 1.0))

            def x_stats(g, q):
                pool.wait_ge(s_x_var, PAIRS * g + q + 1)
                nc.gpsimd.tensor_tensor(x_scale[:, q:q + 1], x_var[:, q:q + 1], neg_half_pow[:], ALU.pow
                                        ).then_inc(s_x_scale, 1)

            def context_stats(c, p):
                pool.wait_ge(s_c_mv, c + 1)
                nc.gpsimd.tensor_tensor(c_sd[:, p:p + 1], c_mv[:, p, 1:2], half_pow[:], ALU.pow).then_inc(s_c_sd, 1)

            def unit(pos, it):
                n = 4 * it + pos
                pool.wait_ge(s_adj_in, 32 * n + 32)
                nc.gpsimd.tensor_tensor(mask[:], mask[:], tri[:].unsqueeze(1).broadcast_to([P, GG, S]),
                                        ALU.mult).then_inc(s_mask, 1)
                if not has_context(pos, it):
                    q = 0
                    for c in range(3 * K, SECOND + WSLOT):
                        while q < PAIRS and (w_slot[c] >= 2 * WSLOT or
                                             (0, x_step(pos, it) + 2 * q) <= LAYER1_STEPS[max(w_before[c] - 3 * K, 0)]):
                            x_stats(prepared_group(pos, it), q)
                            q += 1
                        load_weights(pool, c)
                    assert q == PAIRS
                    return
                for step in range(MB + VH):
                    if step % 2 == 1 and step // 2 < PAIRS:
                        context_stats(4 * (n - 1) + step // 2, step // 2)
                    q, odd = x_turn(pos, it, step)
                    if prepares(pos, it) and not odd and 0 <= q < PAIRS:
                        x_stats(prepared_group(pos, it), q)
                if isinstance(it, int) and n == 1:
                    for c in range(SECOND + WSLOT, WCH):
                        load_weights(pool, c)

            x_stats(0, 0)
            x_stats(0, 1)
            load_weights(pool, WSLOT)
            pool.wait_ge(s_h_lo, 1)
            for c in range(WSLOT + 1, 2 * K):
                load_weights(pool, c)
            x_stats(0, 2)
            x_stats(0, 3)
            for c in range(2 * K, 3 * K):
                load_weights(pool, c)
            all_units(pool, unit)


            def last_times_a(p):
                c = 4 * (4 * ITER - 1) + p
                pool.wait_ge(s_norm, c + 1)
                nc.gpsimd.tensor_tensor(last_rows[p], last_rows[p], a_bc[1][:], ALU.mult).then_inc(s_na, 1)

            pool.wait_ge(s_const, 6 * 16)
            for p in range(PAIRS):
                context_stats(4 * (4 * ITER - 1) + p, p)
                if p == 1:
                    last_times_a(0)
            last_times_a(1)
            last_times_a(2)

        @block.scalar
        def _(act):
            def split_weights(c):
                m, k = c // K, c % K
                act.wait_ge(w_in[c], 16 * w_turn[c])
                nc.scalar.activation(w_hi[m][:, k, :], w_stage[w_slot[c]], ACT.Copy, scale=W_SCALE
                                     ).then_inc(s_w_hi, 1)

            def h_hi_part(rows, u, p):
                act.wait_ge(s_ht[p % 2], 32 * (2 * (u - 1) + p // 2))
                nc.scalar.activation(h_hi[p % 2][:], rows, ACT.Relu).then_inc(s_h_hi, 1)

            def x_norm(g, u, q):
                first = isinstance(g, int) and g == 0
                rows, high = (x_stage[q], first_h[q][0]) if first else (x_in[q % 2][:], h_hi[q % 2][:])
                scale, bias = x_scale[:, q:q + 1], x_bias[:, q:q + 1]
                if not first:
                    wait(act, s_ht[q % 2], 32 * (2 * (u - 1) + q // 2))
                act.wait_ge(s_x_bias, PAIRS * g + q + 1)
                nc.scalar.activation(high, rows, ACT.Relu, scale=scale, bias=bias).then_inc(s_h_hi, 1)
                act.wait_ge(s_h_hi, PAIRS * u + q + 1)
                nc.scalar.activation(rows, rows, ACT.Relu, scale=scale, bias=bias).then_inc(s_x_norm, 1)

            def norm(c, p, slot_wait):
                if p >= 2:
                    act.wait_ge(*slot_wait)
                act.wait_ge(s_c_bias, c + 1)
                for i in range(2):
                    ins = nc.scalar.activation(norm_rows[p % 2][:, i * HALF:(i + 1) * HALF], ps_c[i][:, 0:HALF],
                                               ACT.Identity, scale=c_scale[:, p:p + 1], bias=c_bias[:, p:p + 1])
                ins.then_inc(s_norm, 1)

            def last_norm(p):
                act.wait_ge(s_c_bias, 4 * (4 * ITER - 1) + p + 1)
                for i, bank in enumerate(last_banks(p)):
                    ins = nc.scalar.activation(last_rows[p][:, i * HALF:(i + 1) * HALF], bank[:, 0:HALF],
                                               ACT.Identity, scale=c_scale[:, p:p + 1], bias=c_bias[:, p:p + 1])
                ins.then_inc(s_norm, 1)

            def prepare(pos, it, step):
                q, odd = x_turn(pos, it, step)
                if prepares(pos, it) and odd and 0 <= q < PAIRS:
                    x_norm(prepared_group(pos, it), 4 * it + pos + 1, q)

            def unit(pos, it):
                n = 4 * it + pos
                first = isinstance(it, int) and n == 0
                for j in range(MB):
                    o, side, bank, ended = m_block(first, j)
                    act.wait_ge(s_m, MB * n + ended)
                    if side == 0:
                        wait(act, s_s, K * n + o - 1)
                    nc.scalar.activation(mt_hi[o % 2][:, :, side, :],
                                         bank[:].rearrange("f (g r) -> f g r", r=S), ACT.Copy,
                                         scale=1.0 / W_SCALE).then_inc(s_m_hi, 1)
                    if transposes(pos) and j in (3, 5, 7, 9):
                        p = (j - 3) // 2
                        act.wait_ge(s_nb, 4 * (n - 1) + p + 1)
                        h_hi_part(norm_rows[p % 2][:], n + 1, p)
                    if has_context(pos, it) and j in (2, 4, 6, 8):
                        if isinstance(it, int) and n == 1:
                            act.wait_ge(s_w_lo, SECOND)
                        p = j // 2 - 1
                        norm(4 * (n - 1) + p, p,
                             (s_final, PAIRS * final_group(pos, it) + p - 1) if finals(pos, it) else
                             (s_h_lo, PAIRS * (n + 1) + p - 1))
                    prepare(pos, it, j)
                    for c in chunks_at(pos, it, j):
                        split_weights(c)
                for h in range(VH):
                    act.wait_ge(s_v_sum, VH * n + h + 1)
                    if h == 0:
                        wait(act, s_av, 4 * n)
                    nc.scalar.activation(v_hi[:, h // 2, (h % 2) * HALF:(h % 2 + 1) * HALF], v_sum[h % 2][:],
                                         ACT.Copy).then_inc(s_v_hi, 1)
                    if h == 0:
                        act.wait_ge(s_um, n + 1)
                        nc.scalar.copy(u_shift[0:S, :, :], um[S:P, 0::2, :]).then_inc(s_shift, 1)
                        nc.scalar.copy(u_shift[S:P, :, :], um[0:S, 1::2, :]).then_inc(s_shift, 1)
                        act.wait_ge(s_u, 2 * n + 2)
                        nc.scalar.activation(e_t[:], u_shift[:], ACT.Exp, scale=TEMPER_INV).then_inc(s_exp, 1)
                    prepare(pos, it, MB + h)
                    for c in chunks_at(pos, it, MB + h):
                        split_weights(c)
                    if is_last(pos, it) and h == VH - 1:
                        last_norm(0)

            split_weights(0)
            x_norm(0, 0, 0)
            split_weights(1)
            x_norm(0, 0, 1)
            for c in range(2, K):
                split_weights(c)
            x_norm(0, 0, 2)
            x_norm(0, 0, 3)
            for c in range(K, 3 * K):
                split_weights(c)
            all_units(act, unit)
            for p in range(1, PAIRS):
                last_norm(p)

        @block.vector
        def _(dve):
            def carry_wait():
                nc.vector.memset(carrier[:], 0.0)

            def split_weights(c):
                m, k = c // K, c % K
                dve.wait_ge(s_w_hi, c + 1)
                nc.vector.scalar_tensor_tensor(w_lo[m][:, k, :], w_stage[w_slot[c]], W_SCALE, w_hi[m][:, k, :],
                                               ALU.mult, ALU.subtract).then_inc(s_w_lo, 1)

            def x_row_stats(g, q):
                if isinstance(g, int) and g == 0:
                    rows = x_stage[q]
                    dve.wait_ge(s_x0_in[q], 16)
                else:
                    rows = x_in[q % 2][:]
                    dve.wait_ge(s_x_in[q % 2], 32 * g + 16 * (q // 2) - 16)
                for i in range(2):
                    nc.vector.bn_stats(x_bn[:, q, i, :], rows[:, i * HALF:(i + 1) * HALF]).then_inc(s_x_bn, 1)
                dve.wait_ge(s_x_bn, 8 * g + 2 * q + 2)
                carry_wait()
                nc.vector.bn_aggr(x_mv[:, q, :], x_bn[:, q, :, :].rearrange("p a b -> p (a b)")).then_inc(s_x_mv, 1)
                dve.wait_ge(s_x_mv, PAIRS * g + q + 1)
                nc.vector.tensor_scalar(x_var[:, q:q + 1], x_mv[:, q, 1:2], LN_X_EPS, None, ALU.add
                                        ).then_inc(s_x_var, 1)

            def x_shift(g, q):
                dve.wait_ge(s_x_scale, PAIRS * g + q + 1)
                nc.vector.scalar_tensor_tensor(x_bias[:, q:q + 1], x_mv[:, q, 0:1], -1.0, x_scale[:, q:q + 1],
                                               ALU.mult, ALU.mult).then_inc(s_x_bias, 1)

            def h_lo_part(u, p):
                dve.wait_ge(s_h_hi, PAIRS * u + p + 1)
                nc.vector.scalar_tensor_tensor(h_lo[p % 2][:], norm_rows[p % 2][:], 0.0, h_hi[p % 2][:],
                                               ALU.max, ALU.subtract).then_inc(s_h_lo, 1)

            def x_lo(g, q):
                rows, (high, low) = ((x_stage[q], first_h[q]) if isinstance(g, int) and g == 0 else
                                     (x_in[q % 2][:], (h_hi[q % 2][:], h_lo[q % 2][:])))
                dve.wait_ge(s_x_norm, PAIRS * g + q + 1)
                nc.vector.tensor_tensor(low, rows, high, ALU.subtract).then_inc(s_h_lo, 1)

            def context_stats(c, p, banks=ps_c):
                dve.wait_ge(s_av, c + 1)
                for i in range(2):
                    nc.vector.bn_stats(c_bn[:, p, i, :], banks[i][:, 0:HALF]).then_inc(s_c_bn, 1)
                dve.wait_ge(s_c_bn, 2 * c + 2)
                carry_wait()
                nc.vector.bn_aggr(c_mv[:, p, :], c_bn[:, p, :, :].rearrange("p a b -> p (a b)")).then_inc(s_c_mv, 1)

            def context_scale(c, p):
                dve.wait_ge(s_c_sd, c + 1)
                nc.vector.tensor_scalar(c_den[:, p:p + 1], c_sd[:, p:p + 1], STD_FIX, LN_EPS * ATT_SCALE,
                                        ALU.mult, ALU.add).then_inc(s_c_den, 1)
                dve.wait_ge(s_c_den, c + 1)
                nc.vector.reciprocal(c_scale[:, p:p + 1], c_den[:, p:p + 1]).then_inc(s_c_scale, 1)
                dve.wait_ge(s_c_scale, c + 1)
                nc.vector.scalar_tensor_tensor(c_bias[:, p:p + 1], c_mv[:, p, 0:1], -1.0, c_scale[:, p:p + 1],
                                               ALU.mult, ALU.mult).then_inc(s_c_bias, 1)

            def affine(c, p, layer):
                rows = norm_rows[p % 2]
                dve.wait_ge(s_norm, c + 1)
                nc.vector.tensor_tensor(rows[:], rows[:], a_bc[layer][:], ALU.mult).then_inc(s_na, 1)
                dve.wait_ge(s_na, c + 1)
                nc.vector.tensor_tensor(rows[:], rows[:], b_bc[layer][:], ALU.add).then_inc(s_nb, 1)

            def final(c, G, p):
                affine(c, p, 1)
                res = res_rows[p % 2]
                dve.wait_ge(s_nb, c + 1)
                dve.wait_ge(s_res_in[p % 2], 32 * G + 16 * (p // 2) + 16)
                nc.vector.scalar_tensor_tensor(res[:], norm_rows[p % 2][:], 0.0, res[:], ALU.max, ALU.add
                                               ).then_inc(s_final, 1)

            def v_lo_part(n, h):
                dve.wait_ge(s_v_hi, VH * n + h + 1)
                at = slice((h % 2) * HALF, (h % 2 + 1) * HALF)
                nc.vector.tensor_tensor(v_lo[:, h // 2, at], v_sum[h % 2][:], v_hi[:, h // 2, at], ALU.subtract
                                        ).then_inc(s_v_lo, 1)

            LAST = 4 * (4 * ITER - 1)

            def last_stats(p):
                context_stats(LAST + p, p, last_banks(p))

            def last_scale(p):
                context_scale(LAST + p, p)

            def last_times_a(p):
                dve.wait_ge(s_norm, LAST + p + 1)
                nc.vector.tensor_tensor(last_rows[p], last_rows[p], a_bc[1][:], ALU.mult).then_inc(s_na, 1)

            def last_plus_b(p):
                dve.wait_ge(s_na, LAST + p + 1)
                nc.vector.tensor_tensor(last_rows[p], last_rows[p], b_bc[1][:], ALU.add).then_inc(s_nb, 1)

            def last_plus_x(p):
                res = last_res[p]
                dve.wait_ge(s_nb, LAST + p + 1)
                if p < 2:
                    dve.wait_ge(s_res_in[p], 32 * (NGROUP - 1) + 16)
                else:
                    dve.wait_ge(s_last_res_in[p - 2], 16)
                nc.vector.scalar_tensor_tensor(res, last_rows[p], 0.0, res, ALU.max, ALU.add).then_inc(s_final, 1)

            def prepare(pos, it, step):
                q, odd = x_turn(pos, it, step)
                if prepares(pos, it) and not odd:
                    if 1 <= q <= PAIRS:
                        x_lo(prepared_group(pos, it), q - 1)
                    if 0 <= q < PAIRS:
                        x_row_stats(prepared_group(pos, it), q)

            def prepare_shift(pos, it, step):
                q, odd = x_turn(pos, it, step)
                if prepares(pos, it) and odd and 0 <= q < PAIRS:
                    x_shift(prepared_group(pos, it), q)

            def unit(pos, it):
                n = 4 * it + pos
                layer = pos // 2
                first = isinstance(it, int) and n == 0
                for j in range(MB):
                    o, side, bank, _ = m_block(first, j)
                    dve.wait_ge(s_m_hi, MB * n + j + 1)
                    nc.vector.scalar_tensor_tensor(mt_lo[o % 2][:, :, side, :],
                                                   bank[:].rearrange("f (g r) -> f g r", r=S),
                                                   1.0 / W_SCALE,
                                                   mt_hi[o % 2][:, :, side, :], ALU.mult, ALU.subtract
                                                   ).then_inc(s_m_lo, 1)
                    prepare_shift(pos, it, j)
                    if has_context(pos, it) and j in (2, 4, 6, 8):
                        context_scale(4 * (n - 1) + j // 2 - 1, j // 2 - 1)
                    if has_context(pos, it) and j in (1, 3, 5, 7):
                        context_stats(4 * (n - 1) + j // 2, j // 2)
                    if transposes(pos) and j in (3, 5, 7, 9):
                        affine(4 * (n - 1) + (j - 3) // 2, (j - 3) // 2, 0)
                    if transposes(pos) and j in (4, 6, 8, 10):
                        p = (j - 4) // 2
                        h_lo_part(n + 1, p)
                    if finals(pos, it) and j in (3, 5, 7, 9):
                        p = (j - 3) // 2
                        final(4 * (n - 1) + p, final_group(pos, it), p)
                    prepare(pos, it, j)
                    for c in chunks_at(pos, it, j - 1):
                        split_weights(c)
                for h in range(VH):
                    if h >= 1:
                        v_lo_part(n, h - 1)
                    if is_last(pos, it) and h == VH - 1:
                        last_stats(0)
                        last_scale(0)
                    if first and h == 0:
                        dve.wait_ge(s_const, 6 * 16)
                    dve.wait_ge(s_v, VH * n + h + 1)
                    nc.vector.scalar_tensor_tensor(v_sum[h % 2][:], ps_w[h % 4][:, 0:HALF], 1.0 / W_SCALE,
                                                   b_lin_bc[layer][:, (h % 2) * HALF:(h % 2 + 1) * HALF],
                                                   ALU.mult, ALU.add).then_inc(s_v_sum, 1)
                    prepare_shift(pos, it, MB + h)
                    if h == 0:
                        dve.wait_ge(s_s, K * n + K)
                        dve.wait_ge(s_mask, n + 1)
                        nc.vector.tensor_tensor(um[:], ps_s[:], mask[:], ALU.mult).then_inc(s_um, 1)
                        for s in range(2):
                            at = slice(s * S, (s + 1) * S)
                            dve.wait_ge(s_shift, 2 * n + 1 + s)
                            nc.vector.tensor_tensor(u_shift[at, :, :], um[at, s::2, :], u_shift[at, :, :], ALU.add
                                                    ).then_inc(s_u, 1)
                    if h == 1:
                        dve.wait_ge(s_exp, n + 1)
                        dve.wait_ge(s_adje_in, 32 * n + 32)
                        nc.vector.tensor_tensor(e_t[:], e_t[:], adj_e[:], ALU.mult).then_inc(s_e, 2)
                    if h == 4:
                        dve.wait_ge(s_den, n + 1)
                        nc.vector.tensor_scalar(den[:], ps_x[:, 0:PAIRS * S].rearrange("p (a b) -> p a b", b=S),
                                                DEN_EPS, None, ALU.add).then_inc(s_den_rd, 1)
                        dve.wait_ge(s_den_rd, n + 1)
                        nc.vector.reciprocal(den[:], den[:]).then_inc(s_recip, 1)
                        dve.wait_ge(s_recip, n + 1)
                        nc.vector.scalar_tensor_tensor(e_t[:], e_t[:], ATT_SCALE, den[:], ALU.mult, ALU.mult
                                                       ).then_inc(s_att, 1)
                        dve.wait_ge(s_att, n + 1)
                        for s in range(2):
                            at = slice(s * S, (s + 1) * S)
                            nc.vector.tensor_copy(att_hi[at, :, at], e_t[at, :, :]).then_inc(s_att_hi, 1)
                        for s in range(2):
                            at = slice(s * S, (s + 1) * S)
                            dve.wait_ge(s_att_hi, 2 * n + 1 + s)
                            nc.vector.tensor_tensor(att_lo[at, :, at], e_t[at, :, :], att_hi[at, :, at],
                                                    ALU.subtract).then_inc(s_att_lo, 1)
                    prepare(pos, it, MB + h)
                    for c in chunks_at(pos, it, MB + h - 1):
                        split_weights(c)
                    if is_last(pos, it) and h == VH - 1:
                        last_stats(1)
                v_lo_part(n, VH - 1)
            nc.vector.memset(att_hi[:], 0.0).then_inc(s_clear, 1)
            nc.vector.memset(att_lo[:], 0.0).then_inc(s_clear, 1)
            dve.wait_ge(s_clear, 2)
            x_row_stats(0, 0)
            x_row_stats(0, 1)
            x_shift(0, 0)
            x_shift(0, 1)
            split_weights(0)
            x_lo(0, 0)
            split_weights(1)
            x_lo(0, 1)
            for c in range(2, K):
                split_weights(c)
            x_row_stats(0, 2)
            x_row_stats(0, 3)
            x_shift(0, 2)
            x_shift(0, 3)
            x_lo(0, 2)
            x_lo(0, 3)
            for c in range(K, 3 * K):
                split_weights(c)
            all_units(dve, unit)
            last_stats(2)
            last_scale(1)
            last_stats(3)
            last_plus_b(0)
            last_scale(2)
            last_scale(3)
            last_plus_x(0)
            last_plus_b(1)
            last_plus_x(1)
            last_plus_b(2)
            last_times_a(3)
            last_plus_x(2)
            last_plus_b(3)
            last_plus_x(3)

        @block.tensor
        def _(pe):
            def three_passes(ps, pieces, sem):
                last = len(pieces) - 1
                for i, (st_hi, st_lo, mv_hi, mv_lo) in enumerate(pieces):
                    nc.tensor.matmul(ps, st_hi, mv_hi, start=(i == 0), stop=False)
                    nc.tensor.matmul(ps, st_hi, mv_lo, start=False, stop=False)
                    ins = nc.tensor.matmul(ps, st_lo, mv_hi, start=False, stop=(i == last))
                if sem is not None:
                    ins.then_inc(sem, 1)

            def scores(n, buf, o, first):
                pe.wait_ge(s_m_lo, MB * n + m_read(first, o, 1))
                if o == 0:
                    wait(pe, s_um, n)
                for q in range(GG):
                    at = slice(q * S, (q + 1) * S)
                    m_hi = mt_hi[o % 2][:, q, :, :].rearrange("f s r -> f (s r)")
                    m_lo = mt_lo[o % 2][:, q, :, :].rearrange("f s r -> f (s r)")
                    for i, (m, h) in enumerate(((m_hi, ht_hi), (m_hi, ht_lo), (m_lo, ht_hi))):
                        ins = nc.tensor.matmul(ps_s[:, q, :], m, h[buf][:, o, at],
                                               start=(o == 0 and q == 0 and i == 0), stop=(o == K - 1 and i == 2),
                                               skip_group_check=True)
                ins.then_inc(s_s, 1)

            def context_of(p, banks):
                for i in range(2):
                    at = slice(i * HALF, (i + 1) * HALF)
                    three_passes(banks[i][:, 0:HALF],
                                 [(att_hi[:, p, :], att_lo[:, p, :], v_hi[:, p, at], v_lo[:, p, at])],
                                 s_av if i == 1 else None)

            def context(c, p, n):
                if p == 0:
                    pe.wait_ge(s_att_lo, 2 * n)
                    pe.wait_ge(s_v_lo, VH * n)
                wait(pe, s_norm, c)
                context_of(p, ps_c)

            def last_context(p):
                n = 4 * ITER - 1
                if p == 0:
                    pe.wait_ge(s_att_lo, 2 * n + 2)
                    pe.wait_ge(s_norm, PAIRS * n)
                pe.wait_ge(s_v_lo, VH * n + 2 * (p + 1))
                context_of(p, last_banks(p))

            def unit(pos, it):
                n = 4 * it + pos
                buf = pos % 2
                layer = pos // 2
                first = isinstance(it, int) and n == 0
                hh, hl = ht_hi[buf], ht_lo[buf]
                if first:
                    for p in range(PAIRS):
                        pe.wait_ge(s_ht_first[p], 32)
                        at = slice(p * P, (p + 1) * P)
                        for k in range(K):
                            pe.wait_ge(s_w_lo, k + 1)
                            for o in range(K):
                                of = slice(o * P, (o + 1) * P)
                                bank = (ps_w + ps_c)[o][:, at]
                                nc.tensor.matmul(bank, w_hi[0][:, k, of], hh[:, k, at],
                                                 start=(p == 0 and k == 0), stop=False, skip_group_check=True)
                                nc.tensor.matmul(bank, w_hi[0][:, k, of], hl[:, k, at], start=False, stop=False,
                                                 skip_group_check=True)
                                ins = nc.tensor.matmul(bank, w_lo[0][:, k, of], hh[:, k, at], start=False,
                                                       stop=(k == K - 1), skip_group_check=True)
                                if p == PAIRS - 1 and k == K - 1:
                                    ins.then_inc(s_m, 1)
                    pe.wait_ge(s_w_lo, 2 * K)
                else:
                    for i in range(2):
                        pe.wait_ge(s_ht[i], 64 * n)
                    if layer == 1:
                        pe.wait_ge(s_w_lo, WCH)
                for j in range(MB):
                    o, side = j // 2, j % 2
                    m = 3 * layer + side
                    bank = ps_w[o % 2] if first else ps_w[j % 4]
                    if first:
                        if side == 0:
                            continue
                        pe.wait_ge(s_m_lo, m_read(True, o, 0) if o < 2 else m_read(True, o - 2, 1))
                    elif j < 4:
                        wait(pe, s_v_sum, VH * n - 3 + j)
                    else:
                        pe.wait_ge(s_m_lo, MB * n + j - 3)
                    three_passes(bank[:],
                                 [(w_hi[m][:, k, o * P:(o + 1) * P], w_lo[m][:, k, o * P:(o + 1) * P],
                                   hh[:, k, :], hl[:, k, :]) for k in range(K)], s_m)
                    if side == 1 and o >= 1:
                        scores(n, buf, o - 1, first)
                    if has_context(pos, it) and j in (1, 3, 5, 7):
                        context(4 * (n - 1) + j // 2, j // 2, n)
                if first:
                    pe.wait_ge(s_w_lo, 3 * K)
                for h in range(VH):
                    if h < 4:
                        pe.wait_ge(s_m_lo, MB * n + MB - 3 + h if not first else
                                   m_read(True, K - 2, 1) if h == 0 else MB)
                    else:
                        pe.wait_ge(s_v_sum, VH * n + h - 3)
                    m = 3 * layer + 2
                    rows = slice(h // 2 * P, (h // 2 + 1) * P)
                    cols = slice((h % 2) * HALF, (h % 2 + 1) * HALF)
                    three_passes(ps_w[h % 4][:, 0:HALF],
                                 [(hh[:, k, rows], hl[:, k, rows], w_hi[m][:, k, cols], w_lo[m][:, k, cols])
                                  for k in range(K)], s_v)
                    if h == 0:
                        scores(n, buf, K - 1, first)
                    if h == 3:
                        pe.wait_ge(s_e, 2 * n + 2)
                        wait(pe, s_den_rd, n)
                        nc.tensor.matmul(ps_x[:, 0:PAIRS * S], block_ones[:], e_t[:].rearrange("p a b -> p (a b)"),
                                         start=True, stop=True).then_inc(s_den, 1)
                    if is_last(pos, it) and h >= VH - 2:
                        last_context(h - 6)

            pe.wait_ge(s_setup, 8)
            pe.wait_ge(s_clear, 2)
            all_units(pe, unit)
            last_context(2)
            last_context(3)


def kernel(**inputs):
    import numpy as np
    import concourse.bacc as bacc
    from concourse.bass_utils import run_bass_kernel_spmd

    x = np.asarray(inputs["x"])
    adj = np.asarray(inputs["adj"])
    B, S, H = x.shape
    rows = np.ascontiguousarray(x.reshape(B * S, H))
    wt = np.stack([np.asarray(inputs[f"L0_gnn_{n}"]) for n in ("W_left", "W_right", "W_lin")], axis=1)
    wt = np.ascontiguousarray(wt.transpose(0, 1, 3, 2).reshape(-1, H, H))
    arrays = {
        "x_rows": rows,
        "adj": np.ascontiguousarray(adj),
        "adj_t": np.ascontiguousarray(adj.transpose(0, 2, 1)),
        "w_t": wt,
        "b_lin": np.ascontiguousarray(inputs["L0_gnn_b_lin"]),
        "ln_a": np.ascontiguousarray(inputs["L0_gnn_ln_a"]),
        "ln_b": np.ascontiguousarray(inputs["L0_gnn_ln_b"]),
    }
    nc = bacc.Bacc("TRN2", target_bir_lowering=False, num_devices=1)
    aps = [nc.dram_tensor(n, a.shape, mybir.dt.from_np(a.dtype), kind="ExternalInput").ap() for n, a in arrays.items()]
    out = nc.dram_tensor("out", (B * S, H), F32, kind="ExternalOutput").ap()
    build(nc, *aps, out)
    r = run_bass_kernel_spmd(nc, [arrays], core_ids=[0])
    return r.results[0]["out"].reshape(B, S, H)
```
